# Optimizing a Trainium2 kernel written in Bass

```python
import numpy as np
import jax
import jax.numpy as jnp

def _softmax(x, axis=-1):
    return jax.nn.softmax(x, axis=axis)

def _gelu(x):
    return jax.nn.gelu(x, approximate=True)

def _silu(x):
    return jax.nn.silu(x)

def _sigmoid(x):
    return jax.nn.sigmoid(x)

def _layernorm(x, axis=-1, eps=1e-05):
    m = jnp.mean(x, axis=axis, keepdims=True)
    v = jnp.var(x, axis=axis, keepdims=True)
    return (x - m) / jnp.sqrt(v + eps)

def _scatter_add(tgt, idx, src, axis=0):
    return tgt.at[idx].add(src)

def _segment_sum(src, seg, n):
    return jax.ops.segment_sum(src, seg, n)
kernel_name = 'mk_xattn_ffn_d1_seqx_r8_d5d75f'

def setup_inputs(seed: int=0):
    np.random.seed(seed)
    _w = jnp.asarray

    def _rec_inputs():
        import jax
        import jax.numpy as jnp
        _rk = jax.random.key(seed)
        x = -0.0002928 + 1 * jax.random.normal(jax.random.fold_in(_rk, 1), (8, 56, 128), jnp.float32)
        _lenS = 56 - jax.random.randint(jax.random.fold_in(_rk, 7), (8,), 0, max(1, 56 // 4) + 1, jnp.int32)
        _lenS2 = 1500 - jax.random.randint(jax.random.fold_in(_rk, 8), (8,), 0, max(1, 1500 // 4) + 1, jnp.int32)
        _ctx_1024P = jax.random.normal(jax.random.fold_in(_rk, 11), (8, 16, 128), jnp.float32)
        _ctx_1024c = jax.random.dirichlet(jax.random.fold_in(_rk, 511), 0.3 * jnp.ones((16,), jnp.float32), (8, 1500))
        _ctx_1024t = jnp.einsum('bsk,bkd->bsd', _ctx_1024c, _ctx_1024P)
        _ctx_1024t = _ctx_1024t * jax.lax.rsqrt(jnp.mean(jnp.square(_ctx_1024t)) + 1e-12) * 0.953939
        ctx_1024 = -1.39393e-06 + 0.999914 * (_ctx_1024t + 0.3 * jax.random.normal(jax.random.fold_in(_rk, 611), (8, 1500, 128), jnp.float32))
        return (x, ctx_1024)
    x, ctx_1024 = _rec_inputs()

    def _L0_xattn_setup():
        import jax, jax.numpy as jnp
        import numpy as np
        HEADS = 16
        DIM_HEAD = 64
        QUERY_DIM = 128
        INNER = HEADS * DIM_HEAD
        SCALE = DIM_HEAD ** (-0.5)
        key = jax.random.key(seed)
        ks = jax.random.split(key, 6)
        B, N, M = (2, 256, 256)
        x = jax.random.normal(ks[0], (B, N, QUERY_DIM), dtype=jnp.float32)
        context = jax.random.normal(ks[1], (B, M, QUERY_DIM), dtype=jnp.float32)
        s = QUERY_DIM ** (-0.5)
        Wq = jax.random.normal(ks[2], (QUERY_DIM, INNER), dtype=jnp.float32) * s
        Wk = jax.random.normal(ks[3], (QUERY_DIM, INNER), dtype=jnp.float32) * s
        Wv = jax.random.normal(ks[4], (QUERY_DIM, INNER), dtype=jnp.float32) * s
        Wo = jax.random.normal(ks[5], (INNER, QUERY_DIM), dtype=jnp.float32) * INNER ** (-0.5)
        return {'x': x, 'context': context, 'Wq': Wq, 'Wk': Wk, 'Wv': Wv, 'Wo': Wo}
    _L0_xattn_all = _L0_xattn_setup()
    _L0_xattn_in = {k: v for k, v in _L0_xattn_all.items() if k in ('Wq', 'Wk', 'Wv', 'Wo')}
    del _L0_xattn_all

    def _L0_ffn_setup():
        import jax, jax.numpy as jnp
        import numpy as np
        T, Z, D_DIM = (8, 256, 128)
        N_EXP, P_SLOT, H = (64, 32, 128)
        LN_EPS = 1e-05
        key = jax.random.key(seed)
        k = jax.random.split(key, 5)
        s = 0.02
        return {'x': jax.random.normal(k[0], (T, Z, D_DIM), dtype=jnp.float32), 'phi_w': jax.random.normal(k[1], (N_EXP * P_SLOT, D_DIM), dtype=jnp.float32) * s, 'phi_b': jax.random.normal(k[2], (N_EXP * P_SLOT,), dtype=jnp.float32) * s, 'expert_w': jax.random.normal(k[3], (N_EXP, D_DIM, H), dtype=jnp.float32) * s, 'expert_b': jax.random.normal(k[4], (N_EXP, H), dtype=jnp.float32) * s}
    _L0_ffn_all = _L0_ffn_setup()
    _L0_ffn_in = {k: v for k, v in _L0_ffn_all.items() if k in ('phi_w', 'phi_b', 'expert_w', 'expert_b')}
    del _L0_ffn_all
    return {'x': x, 'ctx_1024': ctx_1024, 'L0_xattn_Wq': _L0_xattn_in['Wq'], 'L0_xattn_Wk': _L0_xattn_in['Wk'], 'L0_xattn_Wv': _L0_xattn_in['Wv'], 'L0_xattn_Wo': _L0_xattn_in['Wo'], 'L0_ffn_phi_w': _L0_ffn_in['phi_w'], 'L0_ffn_phi_b': _L0_ffn_in['phi_b'], 'L0_ffn_expert_w': _L0_ffn_in['expert_w'], 'L0_ffn_expert_b': _L0_ffn_in['expert_b']}

def reference(x, ctx_1024, L0_xattn_Wq, L0_xattn_Wk, L0_xattn_Wv, L0_xattn_Wo, L0_ffn_phi_w, L0_ffn_phi_b, L0_ffn_expert_w, L0_ffn_expert_b):
    import jax
    import jax.numpy as jnp

    def _L0_xattn_ref(x, context, Wq, Wk, Wv, Wo):
        import jax, jax.numpy as jnp
        import numpy as np
        HEADS = 16
        DIM_HEAD = 64
        QUERY_DIM = 128
        INNER = HEADS * DIM_HEAD
        SCALE = DIM_HEAD ** (-0.5)
        B, N, _ = x.shape
        M = context.shape[1]
        q = (x @ Wq).reshape(B, N, HEADS, DIM_HEAD)
        k = (context @ Wk).reshape(B, M, HEADS, DIM_HEAD)
        v = (context @ Wv).reshape(B, M, HEADS, DIM_HEAD)
        sim = jnp.einsum('bihd,bjhd->bhij', q, k) * SCALE
        attn = jax.nn.softmax(sim, axis=-1)
        out = jnp.einsum('bhij,bjhd->bihd', attn, v)
        out = out.reshape(B, N, INNER)
        return out @ Wo

    def _L0_ffn_ref(x, phi_w, phi_b, expert_w, expert_b):
        import jax, jax.numpy as jnp
        import numpy as np
        T, Z, D_DIM = (8, 256, 128)
        N_EXP, P_SLOT, H = (64, 32, 128)
        LN_EPS = 1e-05
        t, z, d = x.shape
        n = expert_w.shape[0]
        p = phi_w.shape[0] // n
        logits = (jnp.einsum('tzd,ed->tze', x, phi_w) + phi_b).reshape(t, z, n, p)
        D = jax.nn.softmax(logits, axis=3)
        C = jax.nn.softmax(logits, axis=2)
        X_tilde = jnp.einsum('tznp,tzd->npd', D, x)
        X_tilde = jnp.clip(X_tilde, -33000.0, 65000.0)
        mu = jnp.mean(X_tilde, axis=-1, keepdims=True)
        var = jnp.mean(jnp.square(X_tilde - mu), axis=-1, keepdims=True)
        X_tilde = (X_tilde - mu) * jax.lax.rsqrt(var + LN_EPS)
        X_tilde = jnp.tanh(X_tilde)
        Y_tilde = jnp.einsum('npd,ndH->npH', X_tilde, expert_w) + expert_b[:, None, :]
        Y = jnp.einsum('tznp,npH->tzH', C, Y_tilde)
        return Y
    x = x + _L0_xattn_ref(_layernorm(x, axis=-1), ctx_1024, L0_xattn_Wq, L0_xattn_Wk, L0_xattn_Wv, L0_xattn_Wo)
    x = x + _L0_ffn_ref(_layernorm(x, axis=-1), L0_ffn_phi_w, L0_ffn_phi_b, L0_ffn_expert_w, L0_ffn_expert_b)
    return x

_drawn_inputs = setup_inputs


def setup_inputs(seed=0):
    import zlib

    import numpy as np

    out = dict(_drawn_inputs(seed))
    spreads = {}
    factors = {'L0_ffn_phi_w': 2.776, 'L0_ffn_phi_b': 29.937}
    for name, (base, spread) in spreads.items():
        noise = np.random.default_rng([zlib.crc32(name.encode()), seed]).standard_normal(out[name].shape)
        drawn = base * np.exp(spread * noise) if base else spread * noise
        out[name] = jnp.asarray(drawn.astype(out[name].dtype))
    for name, factor in factors.items():
        out[name] = (out[name] * factor).astype(out[name].dtype)
    return out
```

```python
from contextlib import ExitStack

import concourse.bass as bass
from concourse import mybir

F32 = mybir.dt.float32
F32R = mybir.dt.float32r
ALU = mybir.AluOpType
ACT = mybir.ActivationFunctionType
AX = mybir.AxisListType


def xattn_softmoe_kernel(
    nc: bass.Bass,
    x: bass.AP,
    ctx_1024: bass.AP,
    Wq: bass.AP,
    Wk: bass.AP,
    Wv: bass.AP,
    Wo: bass.AP,
    phi_w: bass.AP,
    phi_b: bass.AP,
    expert_w: bass.AP,
    expert_b: bass.AP,
    out: bass.AP,
):
    B, T, D = x.shape
    M = ctx_1024.shape[1]
    INNER = Wq.shape[1]
    DH = 64
    HEADS = INNER // DH
    ROWS = HEADS * T
    NT = ROWS // 128
    NC = 12
    CK = M // NC
    KB = 3
    KW = M // KB
    CPB = NC // KB
    PAIRS = B // 2
    PT = 2 * T
    TOK = B * T
    EPS = 1e-5
    SCALE = DH ** -0.5
    N_EXP, _, H = expert_w.shape
    SLOTS = phi_w.shape[0]
    P_SLOT = SLOTS // N_EXP
    NS = SLOTS // 128
    EPT = 128 // P_SLOT
    NQ = TOK // PT
    LC = SLOTS // 512
    assert ROWS == NT * 128 and NT == 7 and M == NC * CK and KW <= 512 and D == 128
    GROUPS = ((0, 3), (3, 7))

    def wait(eng, sem, value):
        if isinstance(value, int) and value <= 0:
            return
        eng.wait_ge(sem, value)

    with ExitStack() as ctx:
        def sem(name):
            return ctx.enter_context(nc.semaphore(name))

        def sb(name, shape, dt=F32, c=ctx):
            return c.enter_context(nc.sbuf_tensor(name, shape, dt))

        scores = ctx.enter_context(nc.psum_tensor("scores", [128, KB, 512], F32))
        turned = ctx.enter_context(nc.psum_tensor("turned", [128, 2, 512], F32))
        acc = ctx.enter_context(nc.psum_tensor("acc", [128, 512], F32))
        misc = ctx.enter_context(nc.psum_tensor("misc", [128, 2, 512], F32))

        ident = sb("ident", [128, 128])
        zero = sb("zero", [128, 1])
        x_sb = sb("x_sb", [PT, NQ, D])
        yT = sb("yT", [D, TOK])
        xnT = sb("xnT", [D, TOK])
        phiT = sb("phiT", [D, SLOTS])
        lnbuf = sb("lnbuf", [PT, NQ, 6])
        lnmv = sb("lnmv", [PT, NQ, 2])
        lnstd = sb("lnstd", [PT, NQ])
        lnrs = sb("lnrs", [PT, NQ])

        attn = ExitStack()
        with attn:
            wqk = sb("wqk", [D, HEADS, D], F32, attn)
            wvo = sb("wvo", [D, HEADS, D], F32, attn)
            ctx_raw = sb("ctx_raw", [CK, NC, D], F32, attn)
            ctx_nh = [sb(f"ctx_nh{a}", [CK, NC, D], F32R, attn) for a in range(2)]
            ctx_nl = [sb(f"ctx_nl{a}", [CK, NC, D], F32R, attn) for a in range(2)]
            ctx_th = [sb(f"ctx_th{a}", [D, M], F32R, attn) for a in range(2)]
            ctx_tl = [sb(f"ctx_tl{a}", [D, M], F32R, attn) for a in range(2)]
            qk_h = [sb(f"qk_h{a}", [D, HEADS, T], F32R, attn) for a in range(2)]
            qk_l = [sb(f"qk_l{a}", [D, HEADS, T], F32R, attn) for a in range(2)]
            qk_raw = sb("qk_raw", [D, HEADS, T], F32, attn)
            prob = [sb(f"prob{a}", [128, M], F32, attn) for a in range(2)]
            bankmax = sb("bankmax", [128, 2, KB], F32, attn)
            negmax = sb("negmax", [128, 2], F32, attn)
            den = sb("den", [128, 2 * NT], F32, attn)
            rden = sb("rden", [128, 2 * NT], F32, attn)
            rbc = sb("rbc", [128, 512], F32, attn)
            oT = sb("oT", [D, 2, HEADS, T], F32, attn)
            oT_cols = oT[:, :, :, :].rearrange("p b h t -> p b (h t)")
            setup = ExitStack()
            with setup:
                wq_sb = sb("wq_sb", [D, INNER], F32, setup)
                wk_sb = sb("wk_sb", [D, INNER], F32, setup)
                wv_sb = sb("wv_sb", [D, INNER], F32, setup)
                wo_sb = sb("wo_sb", [128, HEADS // 2, D], F32, setup)
                wqT = sb("wqT", [128, HEADS // 2, D], F32, setup)
                wkT = sb("wkT", [128, HEADS // 2, D], F32, setup)
                wvT = sb("wvT", [128, HEADS // 2, D], F32, setup)
                phi_sb = sb("phi_sb", [128, NS, D], F32, setup)
                xn = sb("xn", [PT, NQ, D], F32, setup)
            pT_h = sb("pT_h", [128, NT, NC, 128], F32R, attn)
            pT_l = sb("pT_l", [128, NT, NC, 128], F32R, attn)

        moe = ExitStack()
        with moe:
            bias_bc = sb("bias_bc", [PT, SLOTS], F32, moe)
            x1 = sb("x1", [PT, NQ, D], F32, moe)
            x2n = sb("x2n", [PT, NQ, D], F32, moe)
            x2nT = sb("x2nT", [D, TOK], F32, moe)
            logit = [sb(f"logit{a}", [PT, SLOTS], F32, moe) for a in range(2)]
            disp = [sb(f"disp{a}", [PT, SLOTS], F32, moe) for a in range(2)]
            comb = [sb(f"comb{a}", [PT, SLOTS], F32, moe) for a in range(2)]
            dmax = [sb(f"dmax{a}", [PT, N_EXP], F32, moe) for a in range(2)]
            dsum = [sb(f"dsum{a}", [PT, N_EXP], F32, moe) for a in range(2)]
            cmax = [sb(f"cmax{a}", [PT, P_SLOT], F32, moe) for a in range(2)]
            csum = [sb(f"csum{a}", [PT, P_SLOT], F32, moe) for a in range(2)]
            combT = sb("combT", [128, NS, TOK], F32, moe)
            xt = sb("xt", [128, NS, D], F32, moe)
            xtT = sb("xtT", [128, NS, 128], F32, moe)
            xt_st = sb("xt_st", [128, NS, 6], F32, moe)
            xt_mv = sb("xt_mv", [128, NS, 2], F32, moe)
            xt_std = sb("xt_std", [128, NS], F32, moe)
            xt_rs = sb("xt_rs", [128, NS], F32, moe)
            yt = sb("yt", [128, NS, H], F32, moe)
            y2T = sb("y2T", [H, TOK], F32, moe)
            out_sb = sb("out_sb", [PT, NQ, D], F32, moe)
            ew = sb("ew", [D, N_EXP, H], F32, moe)
            eb = sb("eb", [128, NS, H], F32, moe)

        x_in = sem("x_in")
        wqk_in = sem("wqk_in")
        wvo_in = sem("wvo_in")
        phi_in = sem("phi_in")
        zeroed = sem("zeroed")
        ident_ready = sem("ident_ready")
        ln_step = sem("ln_step")
        std_ready = sem("std_ready")
        lnr = sem("lnr")
        xn_ready = sem("xn_ready")
        setup_pe = sem("setup_pe")
        setup_act = sem("setup_act")
        setup_dve = sem("setup_dve")
        ctx_in = sem("ctx_in")
        ctx_nat = sem("ctx_nat")
        nat_hi = sem("nat_hi")
        ctxT_pe = sem("ctxT_pe")
        ctxT_hi = sem("ctxT_hi")
        ctxT_lo = sem("ctxT_lo")
        qk_pe = sem("qk_pe")
        qk_hi = sem("qk_hi")
        qk_lo = sem("qk_lo")
        qkb_hi = sem("qkb_hi")
        qkb_lo = sem("qkb_lo")
        scores_pe = sem("scores_pe")
        bmax_dve = sem("bmax_dve")
        negmax_dve = sem("negmax_dve")
        exp_act = sem("exp_act")
        turned_pe = sem("turned_pe")
        pT_hi = sem("pT_hi")
        pT_lo = sem("pT_lo")
        pv_pe = sem("pv_pe")
        rden_dve = sem("rden_dve")
        rbc_pe = sem("rbc_pe")
        rbc_act = sem("rbc_act")
        oT_dve = sem("oT_dve")
        y_pe = sem("y_pe")
        y_act = sem("y_act")
        bias_in = sem("bias_in")
        ew_in = sem("ew_in")
        eb_in = sem("eb_in")
        yturn_pe = sem("yturn_pe")
        x1_dve = sem("x1_dve")
        x2n_dve = sem("x2n_dve")
        x2nT_pe = sem("x2nT_pe")
        x2nT_act = sem("x2nT_act")
        logit_pe = sem("logit_pe")
        logit_dve = sem("logit_dve")
        dmax_dve = sem("dmax_dve")
        cmax_dve = sem("cmax_dve")
        dsub_pool = sem("dsub_pool")
        csub_dve = sem("csub_dve")
        dexp_act = sem("dexp_act")
        cexp_act = sem("cexp_act")
        dsum_dve = sem("dsum_dve")
        csum_dve = sem("csum_dve")
        drec_dve = sem("drec_dve")
        crec_dve = sem("crec_dve")
        disp_pool = sem("disp_pool")
        comb_pool = sem("comb_pool")
        xt_pe = sem("xt_pe")
        combT_pe = sem("combT_pe")
        combT_act = sem("combT_act")
        clip_dve = sem("clip_dve")
        stat_dve = sem("stat_dve")
        norm_dve = sem("norm_dve")
        tanh_act = sem("tanh_act")
        xtT_pe = sem("xtT_pe")
        xtT_cp = sem("xtT_cp")
        yt_pe = sem("yt_pe")
        yt_dve = sem("yt_dve")
        y2_pe = sem("y2_pe")
        y2_act = sem("y2_act")
        y2turn_pe = sem("y2turn_pe")
        out_dve = sem("out_dve")
        stored = sem("stored")

        ctx_v = ctx_1024.rearrange("b (p j) d -> b p j d", j=NC)
        x_v = x.rearrange("(q b) t d -> (b t) q d", b=2)
        out_v = out.rearrange("(q b) t d -> (b t) q d", b=2)

        def bank(k):
            return [scores[:, 0, :], scores[:, 1, :], scores[:, 2, :], turned[:, 0, :],
                    turned[:, 1, :], acc[:, :], misc[:, 0, :], misc[:, 1, :]][k]

        def heads4(ap, n):
            return ap[:, 0:4 * n].rearrange("p (h c) -> p h c", h=4)

        block = ctx.enter_context(nc.Block())

        @block.sync
        def _(sp):
            sp.dma_start(x_sb[:, :, :], x_v).then_inc(x_in, 16)
            sp.dma_start(wq_sb[:, :], Wq).then_inc(wqk_in, 16)
            sp.dma_start(wk_sb[:, :], Wk).then_inc(wqk_in, 16)
            sp.dma_start(ctx_raw[:, :, :], ctx_v[0]).then_inc(ctx_in, 16)

            def load_ctx(b):
                sp.wait_ge(ctxT_pe, KB * b)
                sp.wait_ge(ctx_nat, b)
                sp.dma_start(ctx_raw[:, :, :], ctx_v[b]).then_inc(ctx_in, 16)

            load_ctx(1)
            with sp.Fori(1, PAIRS) as i:
                load_ctx(2 * i)
                load_ctx(2 * i + 1)

            sp.wait_ge(oT_dve, 2 * B)
            sp.wait_ge(y_act, PAIRS)
            sp.dma_start(bias_bc[:, :], phi_b.partition_broadcast(PT)).then_inc(bias_in, 16)
            sp.dma_start(ew[:, :, :], expert_w.rearrange("n d h -> d n h")).then_inc(ew_in, 16)
            eb_v = expert_b.rearrange("(k n) h -> n k h", n=EPT)
            for n in range(EPT):
                sp.dma_start(eb[n * P_SLOT:(n + 1) * P_SLOT, :, :],
                             eb_v[n].partition_broadcast(P_SLOT)).then_inc(eb_in, 16)
            sp.wait_ge(out_dve, 1)
            sp.dma_start(out_v, out_sb[:, :, :]).then_inc(stored, 16)
            sp.wait_ge(stored, 16)

        @block.gpsimd
        def _(pool):
            nc.gpsimd.memset(ident[:, :], 0.0).then_inc(zeroed, 1)
            nc.gpsimd.memset(zero[:, :], 0.0).then_inc(zeroed, 1)
            pool.wait_ge(zeroed, 2)
            nc.gpsimd.affine_select(out=ident[:, :], in_=ident[:, :], compare_op=ALU.not_equal,
                                    fill=1.0, base=0, pattern=[[-1, 128]],
                                    channel_multiplier=1).then_inc(ident_ready, 1)

            def split_ctx(b, a):
                pool.wait_ge(ctx_in, 16 * (b + 1))
                wait(pool, pv_pe, 2 * (b - 1))
                nc.gpsimd.tensor_tensor(ctx_nh[a][:, :, :].rearrange("p j d -> p (j d)"),
                                        ctx_raw[:, :, :].rearrange("p j d -> p (j d)"),
                                        zero[0:CK, :].broadcast_to([CK, NC * D]), ALU.add).then_inc(nat_hi, 1)
                pool.wait_ge(nat_hi, b + 1)
                nc.gpsimd.tensor_tensor(ctx_nl[a][:, :, :], ctx_raw[:, :, :],
                                        ctx_nh[a][:, :, :].bitcast(F32), ALU.subtract).then_inc(ctx_nat, 1)

            def split_qk(i):
                pool.wait_ge(qk_lo, 4 * (i + 1))
                wait(pool, scores_pe, KB * 2 * NT * i)
                nc.gpsimd.tensor_tensor(qk_h[1][:, :, :].rearrange("p h t -> p (h t)"),
                                        qk_raw[:, :, :].rearrange("p h t -> p (h t)"),
                                        zero[:, :].broadcast_to([D, ROWS]), ALU.add).then_inc(qkb_hi, 1)
                pool.wait_ge(qkb_hi, i + 1)
                nc.gpsimd.tensor_tensor(qk_l[1][:, :, :], qk_raw[:, :, :],
                                        qk_h[1][:, :, :].bitcast(F32), ALU.subtract).then_inc(qkb_lo, 1)

            def pair(i, last=False):
                split_qk(i)
                split_ctx(2 * i + 1, 1)
                if not last:
                    split_ctx(2 * i + 2, 0)

            split_ctx(0, 0)
            pair(0)
            with pool.Fori(1, PAIRS - 1) as i:
                pair(i)
            pair(PAIRS - 1, last=True)

            def by_expert(ap):
                return ap[:, :].rearrange("p (n s) -> p n s", n=N_EXP)

            def dispatch_shift(q):
                a = q % 2
                pool.wait_ge(dmax_dve, q + 1)
                wait(pool, xt_pe, q - 1)
                nc.gpsimd.tensor_tensor(by_expert(disp[a]), by_expert(logit[a]),
                                        dmax[a][:, :].unsqueeze(2).broadcast_to([PT, N_EXP, P_SLOT]),
                                        ALU.subtract).then_inc(dsub_pool, 1)

            dispatch_shift(0)
            for q in range(NQ):
                a = q % 2
                if q + 1 < NQ:
                    dispatch_shift(q + 1)
                pool.wait_ge(drec_dve, q + 1)
                nc.gpsimd.tensor_tensor(by_expert(disp[a]), by_expert(disp[a]),
                                        dsum[a][:, :].unsqueeze(2).broadcast_to([PT, N_EXP, P_SLOT]),
                                        ALU.mult).then_inc(disp_pool, 1)
                pool.wait_ge(crec_dve, q + 1)
                nc.gpsimd.tensor_tensor(by_expert(comb[a]), by_expert(comb[a]),
                                        csum[a][:, :].unsqueeze(1).broadcast_to([PT, N_EXP, P_SLOT]),
                                        ALU.mult).then_inc(comb_pool, 1)

        @block.tensor
        def _(pe):
            mm = nc.tensor.matmul
            tr = nc.tensor.transpose

            pe.wait_ge(ident_ready, 1)

            def turn_weight(w, half, k):
                for c in range(4):
                    j = 4 * half + c
                    last = tr(bank(k)[:, 128 * c:128 * c + 128], w[:, 128 * j:128 * j + 128], ident[:, :])
                last.then_inc(setup_pe, 1)

            def head_products(wT, right, r, k):
                p = DH * (r % 2)
                for c in range(4):
                    j = r // 2 * 4 + c
                    last = mm(bank(k)[:, 128 * c:128 * c + 128], wT[p:p + DH, j, :],
                              right[p:p + DH, j, :], start=True, stop=True)
                last.then_inc(setup_pe, 1)

            pe.wait_ge(wqk_in, 32)
            turn_weight(wq_sb, 0, 0)
            turn_weight(wq_sb, 1, 1)
            turn_weight(wk_sb, 0, 2)
            turn_weight(wk_sb, 1, 3)
            pe.wait_ge(setup_dve, 2)
            head_products(wqT, wkT, 0, 4)
            head_products(wqT, wkT, 1, 5)
            pe.wait_ge(setup_act, 2)
            head_products(wqT, wkT, 2, 0)
            head_products(wqT, wkT, 3, 1)
            pe.wait_ge(xn_ready, NQ)
            for q in range(NQ):
                last = tr(bank(2)[:, PT * q:PT * q + PT], xn[:, q, :], ident[0:PT, 0:PT])
            last.then_inc(setup_pe, 1)
            pe.wait_ge(wvo_in, 32)
            turn_weight(wv_sb, 0, 3)
            pe.wait_ge(setup_act, 3)
            turn_weight(wv_sb, 1, 4)
            pe.wait_ge(setup_dve, 5)
            head_products(wvT, wo_sb, 0, 5)
            pe.wait_ge(setup_act, 4)
            head_products(wvT, wo_sb, 1, 0)
            pe.wait_ge(setup_act, 5)
            head_products(wvT, wo_sb, 2, 1)
            head_products(wvT, wo_sb, 3, 2)
            pe.wait_ge(phi_in, 16)
            pe.wait_ge(setup_dve, 6)
            for r, k in enumerate((3, 4, 5, 6)):
                for c in range(4):
                    last = tr(bank(k)[:, 128 * c:128 * c + 128], phi_sb[:, 4 * r + c, :], ident[:, :])
                last.then_inc(setup_pe, 1)
            pe.wait_ge(setup_act, 9)
            pe.wait_ge(setup_dve, 10)

            def turn_ctx(b, k, m):
                pe.wait_ge(ctx_in, 16 * (b + 1))
                for c in range(CPB):
                    last = tr(misc[:, m, CK * c:CK * c + CK], ctx_raw[:, CPB * k + c, :], ident[0:CK, 0:CK])
                last.then_inc(ctxT_pe, 1)

            def make_qk(i, r, m):
                for c in range(4):
                    last = mm(misc[:, m, PT * c:PT * c + PT], wqk[:, 4 * r + c, :],
                              xnT[:, bass.ds(i * PT, PT)], start=True, stop=True)
                last.then_inc(qk_pe, 1)

            def make_scores(g, a, t):
                wait(pe, exp_act, g)
                rows = slice(128 * t, 128 * t + 128)
                hi = qk_h[a][:, :, :].rearrange("p h t -> p (h t)")[:, rows]
                lo = qk_l[a][:, :, :].rearrange("p h t -> p (h t)")[:, rows]
                for k in range(KB):
                    o = scores[:, k, 0:KW]
                    keys = slice(KW * k, KW * k + KW)
                    mm(o, hi, ctx_th[a][:, keys], start=True, stop=False)
                    mm(o, hi, ctx_tl[a][:, keys], start=False, stop=False)
                    mm(o, lo, ctx_th[a][:, keys], start=False, stop=True).then_inc(scores_pe, 1)

            def turn_probs(g, u, k):
                m = (KB * u + k) % 2
                wait(pe, pT_lo, KB * g + k - 1)
                if k == 0:
                    pe.wait_ge(exp_act, g + 1)
                for c in range(CPB):
                    j = CPB * k + c
                    last = tr(turned[0:CK, m, 128 * c:128 * c + 128], prob[u][:, CK * j:CK * j + CK],
                              ident[:, :])
                last.then_inc(turned_pe, 1)

            def context_product(b, a, grp, chunks):
                t0, t1 = GROUPS[grp]
                o = acc[:, 0:128 * (t1 - t0)].rearrange("p (t r) -> p t r", r=128)
                for j in chunks:
                    hi, lo = pT_h[0:CK, t0:t1, j, :], pT_l[0:CK, t0:t1, j, :]
                    mm(o, ctx_nh[a][:, j, :], hi, start=(j == 0), stop=False)
                    mm(o, ctx_nh[a][:, j, :], lo, start=False, stop=False)
                    last = mm(o, ctx_nl[a][:, j, :], hi, start=False, stop=(j == NC - 1))
                return last

            def spread_rden(a, grp, m):
                t0, t1 = GROUPS[grp]
                for t in range(t0, t1):
                    last = tr(misc[:, m, 128 * (t - t0):128 * (t - t0) + 128],
                              rden[:, a * NT + t:a * NT + t + 1].broadcast_to([128, 128]), ident[:, :])
                last.then_inc(rbc_pe, 1)

            def project(r):
                for h in range(8 * r, 8 * r + 8):
                    last = mm(misc[:, 0, 0:PT].rearrange("p (b t) -> p b t", b=2), wvo[:, h, :],
                              oT[:, :, h, :], start=(h == 0), stop=(h == HEADS - 1))
                return last

            def half(i, a, first=False, last=False):
                b = i * 2 + a
                for t in range(NT):
                    g = b * NT + t
                    if t == 0:
                        pe.wait_ge(ctxT_lo, KB * (b + 1))
                        if a == 0:
                            pe.wait_ge(qk_lo, (i + 1) * 4)
                        else:
                            pe.wait_ge(qkb_lo, i + 1)
                    make_scores(g, a, t)
                    u = (a + t + 1) % 2
                    chunks, grp, pb, pa = None, 0, 0, 0
                    if 1 <= t <= 3 and not first:
                        chunks, grp, pb, pa = range(4 * t - 4, 4 * t), 1, b - 1, 1 - a
                    if t >= 4:
                        chunks, grp, pb, pa = range(4 * t - 16, 4 * t - 12), 0, b, a
                    if not (first and t == 0):
                        turn_probs(g - 1, u, 0)
                        turn_probs(g - 1, u, 1)
                    if chunks is not None:
                        if chunks[0] == 0:
                            t1 = GROUPS[grp][1]
                            pe.wait_ge(pT_lo, KB * (pb * NT + t1))
                            pe.wait_ge(ctx_nat, pb + 1)
                            wait(pe, oT_dve, pb * 2 + grp)
                        context_product(pb, pa, grp, chunks[0:2])
                    if not (first and t == 0):
                        turn_probs(g - 1, u, 2)
                    if chunks is not None:
                        p = context_product(pb, pa, grp, chunks[2:4])
                        if chunks[-1] == NC - 1:
                            p.then_inc(pv_pe, 1)
                    if t == 0 and a == 1 and not last:
                        wait(pe, y_act, i)
                        pe.wait_ge(ctxT_lo, KB * (b + 0) + 2)
                        make_qk(i + 1, 0, 0)
                        pe.wait_ge(rbc_act, b * 2 - 1)
                        make_qk(i + 1, 1, 1)
                    if t == 1 and not first:
                        pe.wait_ge(rden_dve, b * 2)
                        if a == 0:
                            pe.wait_ge(rbc_act, b * 2 - 1)
                        elif not last:
                            pe.wait_ge(qk_lo, (i + 1) * 4 + 1)
                        else:
                            pe.wait_ge(y_act, i)
                        spread_rden(1 - a, 1, 0)
                        if a == 1 and not last:
                            pe.wait_ge(qk_lo, (i + 1) * 4 + 2)
                            make_qk(i + 1, 2, 1)
                    if 2 <= t <= 4 and not last:
                        k = t - 2
                        if k == 2:
                            pe.wait_ge(ctxT_lo, KB * (b + 1) + 1)
                        elif k == a:
                            wait(pe, rbc_act, b * 2)
                        else:
                            if a == 0:
                                pe.wait_ge(qk_lo, (i + 1) * 4)
                            else:
                                pe.wait_ge(qk_lo, (i + 1) * 4 + 3)
                        turn_ctx(b + 1, k, (1 + k + a) % 2)
                    if a == 0 and t == 5 and not first:
                        pe.wait_ge(oT_dve, b * 2)
                        pe.wait_ge(ctxT_lo, KB * (b + 1) + 2)
                        project(0)
                    if a == 1 and t == 5 and not last:
                        pe.wait_ge(ctxT_lo, KB * (b + 1) + 2)
                        make_qk(i + 1, 3, 1)
                    if t == 6:
                        if a == 0 and not first:
                            project(1).then_inc(y_pe, 1)
                        pe.wait_ge(rden_dve, b * 2 + 1)
                        if not last:
                            pe.wait_ge(ctxT_lo, KB * (b + 1) + 3)
                        spread_rden(a, 0, 1 - a)

            for r in range(2):
                make_qk(0, r, 1 - r)
            for k in range(KB):
                if k == 0:
                    pe.wait_ge(qk_lo, 1)
                elif k == 1:
                    pe.wait_ge(qk_lo, 2)
                else:
                    pe.wait_ge(ctxT_lo, 1)
                turn_ctx(0, k, (1 + k) % 2)
            pe.wait_ge(ctxT_lo, 2)
            make_qk(0, 2, 0)
            pe.wait_ge(ctxT_lo, 3)
            make_qk(0, 3, 1)

            half(0, 0, first=True)
            half(0, 1)
            with pe.Fori(1, PAIRS - 1) as i:
                half(i, 0)
                half(i, 1)
            half(PAIRS - 1, 0)
            half(PAIRS - 1, 1, last=True)
            G = B * NT
            for k in range(KB):
                turn_probs(G - 1, 1, k)
            pe.wait_ge(rden_dve, 2 * B)
            pe.wait_ge(rbc_act, 2 * B - 1)
            spread_rden(1, 1, 0)
            pe.wait_ge(pT_lo, KB * G)
            pe.wait_ge(oT_dve, 2 * B - 1)
            context_product(B - 1, 1, 1, range(NC)).then_inc(pv_pe, 1)
            pe.wait_ge(oT_dve, 2 * B)
            pe.wait_ge(rbc_act, 2 * B)
            project(0)
            project(1).then_inc(y_pe, 1)

            pe.wait_ge(y_act, PAIRS)
            for q in range(NQ):
                last = tr(misc[0:PT, 1, D * q:D * q + D], yT[:, PT * q:PT * q + PT], ident[:, :])
            last.then_inc(yturn_pe, 1)
            pe.wait_ge(x2n_dve, NQ)
            for q in range(NQ):
                last = tr(misc[:, 0, PT * q:PT * q + PT], x2n[:, q, :], ident[0:PT, 0:PT])
            last.then_inc(x2nT_pe, 1)
            pe.wait_ge(x2nT_act, 1)

            def logits(q):
                for c in range(LC):
                    n = LC * q + c
                    wait(pe, logit_dve, n - 1)
                    mm(turned[0:PT, n % 2, :], x2nT[:, PT * q:PT * q + PT], phiT[:, 512 * c:512 * c + 512],
                       start=True, stop=True).then_inc(logit_pe, 1)

            xt_banks = (0, 1, 2, 5)

            def slots_in(q):
                pe.wait_ge(disp_pool, q + 1)
                for k in range(NS):
                    last = mm(bank(xt_banks[k // 4])[:, 128 * (k % 4):128 * (k % 4) + 128],
                              disp[q % 2][:, 128 * k:128 * k + 128], x2n[:, q, :],
                              start=(q == 0 and k % 4 == 0), stop=(q == NQ - 1),
                              skip_group_check=True)
                last.then_inc(xt_pe, 1)

            def turn_comb(q):
                pe.wait_ge(comb_pool, q + 1)
                for r in range(NS // 4):
                    n = NS // 4 * q + r
                    wait(pe, combT_act, n - 1)
                    for c in range(4):
                        k = 4 * r + c
                        last = tr(misc[:, n % 2, PT * c:PT * c + PT], comb[q % 2][:, 128 * k:128 * k + 128],
                                  ident[0:PT, 0:PT])
                    last.then_inc(combT_pe, 1)

            logits(0)
            logits(1)
            for q in range(NQ):
                slots_in(q)
                turn_comb(q)
                if q + 2 < NQ:
                    logits(q + 2)

            for r in range(NS // 4):
                pe.wait_ge(tanh_act, 4 * r + 4)
                wait(pe, xtT_cp, r - 1)
                for c in range(4):
                    last = tr(turned[:, r % 2, 128 * c:128 * c + 128], xt[:, 4 * r + c, :], ident[:, :])
                last.then_inc(xtT_pe, 1)
            pe.wait_ge(ew_in, 16)
            for k in range(NS):
                if k % 4 == 0:
                    pe.wait_ge(xtT_cp, k // 4 + 1)
                for e in range(EPT):
                    s = slice(P_SLOT * e, P_SLOT * e + P_SLOT)
                    last = mm(bank(xt_banks[k // 4])[s, 128 * (k % 4):128 * (k % 4) + 128],
                              xtT[:, k, s], ew[:, EPT * k + e, :], start=True, stop=True)
                if k % 4 == 3:
                    last.then_inc(yt_pe, 1)
            for k in range(NS):
                if k % 4 == 0:
                    pe.wait_ge(yt_dve, k // 4 + 1)
                if k == 0:
                    pe.wait_ge(xtT_cp, 4)
                    pe.wait_ge(combT_act, NS)
                last = mm(turned[:, 0, 0:TOK], yt[:, k, :], combT[:, k, :], start=(k == 0), stop=(k == NS - 1))
            last.then_inc(y2_pe, 1)
            pe.wait_ge(y2_act, 1)
            for q in range(NQ):
                last = tr(misc[0:PT, 0, D * q:D * q + D], y2T[:, PT * q:PT * q + PT], ident[:, :])
            last.then_inc(y2turn_pe, 1)

        @block.scalar
        def _(act):
            act.dma_start(wv_sb[:, :], Wv).then_inc(wvo_in, 16)
            act.dma_start(wo_sb[:, :, :], Wo.rearrange("(j p) n -> p j n", p=128)).then_inc(wvo_in, 16)
            act.dma_start(phi_sb[:, :, :], phi_w.rearrange("(k p) d -> p k d", p=128)).then_inc(phi_in, 16)
            act.wait_ge(ln_step, NQ + NQ + 1)
            nc.scalar.activation(lnstd[:, :], lnstd[:, :], ACT.Sqrt).then_inc(std_ready, 1)

            def copy_out(n, dst, k, width=512):
                act.wait_ge(setup_pe, n)
                return nc.scalar.copy(dst, bank(k)[:, 0:width].rearrange("p (c w) -> p c w", c=4))

            copy_out(2, wqT[:, 4:8, :], 1).then_inc(setup_act, 1)
            copy_out(4, wkT[:, 4:8, :], 3).then_inc(setup_act, 1)
            act.wait_ge(setup_pe, 5)
            nc.scalar.mul(wqk[:, 0:8:2, :], heads4(bank(4), 128), SCALE).then_inc(setup_act, 1)
            act.wait_ge(setup_pe, 7)
            nc.scalar.mul(wqk[:, 8:16:2, :], heads4(bank(0), 128), SCALE).then_inc(setup_act, 1)
            copy_out(11, wvT[:, 4:8, :], 4).then_inc(setup_act, 1)
            copy_out(13, wvo[:, 1:8:2, :], 0).then_inc(setup_act, 1)
            copy_out(15, wvo[:, 9:16:2, :], 2).then_inc(setup_act, 1)
            for n, k, r in ((17, 4, 1), (19, 6, 3)):
                act.wait_ge(setup_pe, n)
                nc.scalar.copy(phiT[:, 512 * r:512 * r + 512], bank(k)).then_inc(setup_act, 1)

            def hi_ctx(b, a, k, m):
                act.wait_ge(ctxT_pe, KB * b + (k + 1))
                nc.scalar.copy(ctx_th[a][:, KW * k:KW * k + KW], misc[:, m, 0:KW]).then_inc(ctxT_hi, 1)

            def hi_qk(i, r, m):
                act.wait_ge(qk_pe, i * 4 + (r + 1))
                if r == 0:
                    wait(act, qkb_lo, i)
                both = misc[:, m, 0:4 * PT].rearrange("p (h b t) -> p b h t", h=4, b=2)
                nc.scalar.copy(qk_raw[:, 4 * r:4 * r + 4, :], both[:, 1])
                nc.scalar.copy(qk_h[0][:, 4 * r:4 * r + 4, :], both[:, 0]).then_inc(qk_hi, 1)

            def hi_probs(g, u, t, k):
                act.wait_ge(turned_pe, KB * g + (k + 1))
                nc.scalar.copy(pT_h[0:CK, t, CPB * k:CPB * k + CPB, :],
                               turned[0:CK, (KB * u + k) % 2, :].rearrange("p (c r) -> p c r", c=CPB)
                               ).then_inc(pT_hi, 1)

            def exp_tile(g, u, a, t):
                act.wait_ge(negmax_dve, g + 1)
                nc.scalar.activation(prob[u][:, :].rearrange("p (k w) -> p k w", k=KB), scores[:, :, 0:KW],
                                     ACT.Exp, bias=negmax[:, u:u + 1],
                                     accum_out=den[:, a * NT + t:a * NT + t + 1]).then_inc(exp_act, 1)

            def copy_rbc(n, grp, m):
                act.wait_ge(rbc_pe, n)
                wait(act, oT_dve, n - 1)
                w = 128 * (GROUPS[grp][1] - GROUPS[grp][0])
                nc.scalar.copy(rbc[:, 0:w], misc[:, m, 0:w]).then_inc(rbc_act, 1)

            def copy_y(i):
                act.wait_ge(y_pe, i + 1)
                nc.scalar.copy(yT[:, bass.ds(i * PT, PT)], misc[:, 0, 0:PT]).then_inc(y_act, 1)

            def half(i, a, first=False, last=False):
                b = i * 2 + a
                for t in range(NT):
                    g = b * NT + t
                    u = (a + t) % 2
                    before = not (first and t == 0)
                    if before:
                        hi_probs(g - 1, 1 - u, (t - 1) % NT, 0)
                    exp_tile(g, u, a, t)
                    if before:
                        hi_probs(g - 1, 1 - u, (t - 1) % NT, 1)
                        hi_probs(g - 1, 1 - u, (t - 1) % NT, 2)
                    if t == 0 and a == 1 and not last:
                        hi_qk(i + 1, 0, 0)
                        hi_qk(i + 1, 1, 1)
                    if t == 1 and not first:
                        copy_rbc(b * 2, 1, 0)
                        if a == 1 and not last:
                            hi_qk(i + 1, 2, 1)
                    if 2 <= t <= 4 and not last:
                        hi_ctx(b + 1, 1 - a, t - 2, (t - 1 + a) % 2)
                    if a == 1 and t == 5 and not last:
                        hi_qk(i + 1, 3, 1)
                    if t == 6:
                        if a == 0 and not first:
                            copy_y(i - 1)
                        copy_rbc(b * 2 + 1, 0, 1 - a)

            hi_qk(0, 0, 1)
            hi_qk(0, 1, 0)
            for k in range(KB):
                hi_ctx(0, 0, k, (1 + k) % 2)
            hi_qk(0, 2, 0)
            hi_qk(0, 3, 1)
            half(0, 0, first=True)
            half(0, 1)
            with act.Fori(1, PAIRS - 1) as i:
                half(i, 0)
                half(i, 1)
            half(PAIRS - 1, 0)
            half(PAIRS - 1, 1, last=True)
            for k in range(KB):
                hi_probs(B * NT - 1, 1, NT - 1, k)
            copy_rbc(2 * B, 1, 0)
            copy_y(PAIRS - 1)

            act.wait_ge(ln_step, 2 * (NQ + NQ + 1))
            nc.scalar.activation(lnstd[:, :], lnstd[:, :], ACT.Sqrt).then_inc(std_ready, 1)
            act.wait_ge(x2nT_pe, 1)
            nc.scalar.copy(x2nT[:, :], misc[:, 0, 0:TOK]).then_inc(x2nT_act, 1)
            for q in range(NQ):
                a = q % 2
                act.wait_ge(dsub_pool, q + 1)
                nc.scalar.activation(disp[a][:, :], disp[a][:, :], ACT.Exp).then_inc(dexp_act, 1)
                act.wait_ge(csub_dve, q + 1)
                nc.scalar.activation(comb[a][:, :], comb[a][:, :], ACT.Exp).then_inc(cexp_act, 1)
                if q >= 1:
                    for r in range(NS // 4):
                        n = NS // 4 * (q - 1) + r
                        act.wait_ge(combT_pe, n + 1)
                        nc.scalar.copy(combT[:, 4 * r:4 * r + 4, PT * (q - 1):PT * q],
                                       misc[:, n % 2, 0:4 * PT].rearrange("p (c t) -> p c t", c=4)
                                       ).then_inc(combT_act, 1)
            for r in range(NS // 4):
                n = NS // 4 * (NQ - 1) + r
                act.wait_ge(combT_pe, n + 1)
                nc.scalar.copy(combT[:, 4 * r:4 * r + 4, PT * (NQ - 1):PT * NQ],
                               misc[:, n % 2, 0:4 * PT].rearrange("p (c t) -> p c t", c=4)
                               ).then_inc(combT_act, 1)
            act.wait_ge(stat_dve, 3)
            nc.scalar.activation(xt_std[:, :], xt_std[:, :], ACT.Sqrt).then_inc(std_ready, 1)
            for k in range(NS):
                act.wait_ge(norm_dve, k + 1)
                nc.scalar.activation(xt[:, k, :], xt[:, k, :], ACT.Tanh).then_inc(tanh_act, 1)
            for r in range(NS // 4):
                act.wait_ge(xtT_pe, r + 1)
                nc.scalar.copy(xtT[:, 4 * r:4 * r + 4, :],
                               turned[:, r % 2, :].rearrange("p (c w) -> p c w", c=4)).then_inc(xtT_cp, 1)
            act.wait_ge(y2_pe, 1)
            nc.scalar.copy(y2T[:, :], turned[:, 0, 0:TOK]).then_inc(y2_act, 1)

        @block.vector
        def _(dve):
            v = nc.vector
            LN = NQ + NQ + 1

            def layernorm(src, dst, n, done):
                for q in range(NQ):
                    v.bn_stats(lnbuf[:, q, :], src[:, q, :]).then_inc(ln_step, 1)
                for q in range(NQ):
                    dve.wait_ge(ln_step, LN * n + q + 1)
                    v.bn_aggr(lnmv[:, q, :], lnbuf[:, q, :]).then_inc(ln_step, 1)
                dve.wait_ge(ln_step, LN * n + 2 * NQ)
                v.tensor_scalar_add(lnstd[:, :], lnmv[:, :, 1], EPS).then_inc(ln_step, 1)
                dve.wait_ge(std_ready, n + 1)
                v.reciprocal(lnrs[:, :], lnstd[:, :]).then_inc(lnr, 1)
                dve.wait_ge(lnr, n + 1)
                for q in range(NQ):
                    v.tensor_scalar(dst[:, q, :], src[:, q, :], lnmv[:, q, 0:1], lnrs[:, q:q + 1],
                                    ALU.subtract, ALU.mult).then_inc(done, 1)

            dve.wait_ge(x_in, 16)
            layernorm(x_sb, xn, 0, xn_ready)

            def copy_out(n, dst, k):
                dve.wait_ge(setup_pe, n)
                return v.tensor_copy(dst, heads4(bank(k), 128))

            copy_out(1, wqT[:, 0:4, :], 0).then_inc(setup_dve, 1)
            copy_out(3, wkT[:, 0:4, :], 2).then_inc(setup_dve, 1)
            dve.wait_ge(setup_pe, 6)
            v.tensor_scalar(wqk[:, 1:8:2, :], heads4(bank(5), 128), SCALE, None, ALU.mult).then_inc(setup_dve, 1)
            dve.wait_ge(setup_pe, 8)
            v.tensor_scalar(wqk[:, 9:16:2, :], heads4(bank(1), 128), SCALE, None, ALU.mult).then_inc(setup_dve, 1)
            dve.wait_ge(setup_pe, 10)
            v.tensor_copy(xnT[:, :], bank(2)[:, 0:TOK])
            v.tensor_copy(wvT[:, 0:4, :], heads4(bank(3), 128)).then_inc(setup_dve, 1)
            copy_out(12, wvo[:, 0:8:2, :], 5).then_inc(setup_dve, 1)
            copy_out(14, wvo[:, 8:16:2, :], 1).then_inc(setup_dve, 1)
            for n, k, r in ((16, 3, 0), (18, 5, 2)):
                dve.wait_ge(setup_pe, n)
                v.tensor_copy(phiT[:, 512 * r:512 * r + 512], bank(k)).then_inc(setup_dve, 1)
            v.memset(den[:, :], 1.0).then_inc(setup_dve, 1)

            def lo_ctx(b, a, k, m):
                dve.wait_ge(ctxT_hi, KB * b + (k + 1))
                cols = slice(KW * k, KW * k + KW)
                v.tensor_tensor(ctx_tl[a][:, cols], misc[:, m, 0:KW], ctx_th[a][:, cols].bitcast(F32),
                                ALU.subtract).then_inc(ctxT_lo, 1)

            def lo_qk(i, r, m):
                dve.wait_ge(qk_hi, i * 4 + (r + 1))
                both = misc[:, m, 0:4 * PT].rearrange("p (h b t) -> p b h t", h=4, b=2)
                hs = slice(4 * r, 4 * r + 4)
                v.tensor_tensor(qk_l[0][:, hs, :], both[:, 0], qk_h[0][:, hs, :].bitcast(F32),
                                ALU.subtract).then_inc(qk_lo, 1)

            def row_max(g, u):
                for k in range(KB):
                    dve.wait_ge(scores_pe, KB * g + (k + 1))
                    m = v.tensor_reduce(bankmax[:, u, k:k + 1], scores[:, k, 0:KW], AX.X, ALU.max)
                m.then_inc(bmax_dve, 1)
                dve.wait_ge(bmax_dve, g + 1)
                v.tensor_reduce(negmax[:, u:u + 1], bankmax[:, u, :], AX.X, ALU.max,
                                negate=True).then_inc(negmax_dve, 1)

            def lo_probs(g, u, t, k):
                dve.wait_ge(pT_hi, KB * g + (k + 1))
                dst = slice(CPB * k, CPB * k + CPB)
                v.tensor_tensor(pT_l[0:CK, t, dst, :],
                                turned[0:CK, (KB * u + k) % 2, :].rearrange("p (c r) -> p c r", c=CPB),
                                pT_h[0:CK, t, dst, :].bitcast(F32), ALU.subtract).then_inc(pT_lo, 1)

            def invert(n, g, a, grp):
                t0, t1 = GROUPS[grp]
                dve.wait_ge(exp_act, g)
                v.reciprocal(rden[:, a * NT + t0:a * NT + t1], den[:, a * NT + t0:a * NT + t1]
                             ).then_inc(rden_dve, 1)

            def normalise(n, a, grp):
                dve.wait_ge(rbc_act, n)
                dve.wait_ge(pv_pe, n)
                t0, t1 = GROUPS[grp]
                w = 128 * (t1 - t0)
                v.tensor_tensor(oT_cols[:, a, 128 * t0:128 * t1], acc[:, 0:w], rbc[:, 0:w],
                                ALU.mult).then_inc(oT_dve, 1)

            def half(i, a, first=False, last=False):
                b = i * 2 + a
                for t in range(NT):
                    g = b * NT + t
                    u = (a + t) % 2
                    if t == 0 and not first:
                        normalise(b * 2 - 1, 1 - a, 0)
                    if t == 4 and not first:
                        normalise(b * 2, 1 - a, 1)
                    row_max(g, u)
                    if not (first and t == 0):
                        for k in range(KB):
                            lo_probs(g - 1, 1 - u, (t - 1) % NT, k)
                    if t == 0 and a == 1 and not last:
                        lo_qk(i + 1, 0, 0)
                        lo_qk(i + 1, 1, 1)
                    if t == 1 and not first:
                        invert(b * 2, b * NT, 1 - a, 1)
                        if a == 1 and not last:
                            lo_qk(i + 1, 2, 1)
                    if 2 <= t <= 4 and not last:
                        lo_ctx(b + 1, 1 - a, t - 2, (t - 1 + a) % 2)
                    if a == 1 and t == 5 and not last:
                        lo_qk(i + 1, 3, 1)
                    if t == 5:
                        invert(b * 2 + 1, b * NT + 3, a, 0)

            lo_qk(0, 0, 1)
            lo_qk(0, 1, 0)
            for k in range(KB):
                lo_ctx(0, 0, k, (1 + k) % 2)
            lo_qk(0, 2, 0)
            lo_qk(0, 3, 1)
            half(0, 0, first=True)
            half(0, 1)
            with dve.Fori(1, PAIRS - 1) as i:
                half(i, 0)
                half(i, 1)
            half(PAIRS - 1, 0)
            half(PAIRS - 1, 1, last=True)
            invert(2 * B, B * NT, 1, 1)
            for k in range(KB):
                lo_probs(B * NT - 1, 1, NT - 1, k)
            normalise(2 * B - 1, 1, 0)
            normalise(2 * B, 1, 1)

            dve.wait_ge(yturn_pe, 1)
            v.tensor_tensor(x1[:, :, :], x_sb[:, :, :], misc[0:PT, 1, :].rearrange("p (q d) -> p q d", q=NQ),
                            ALU.add).then_inc(x1_dve, 1)
            dve.wait_ge(x1_dve, 1)
            layernorm(x1, x2n, 1, x2n_dve)

            def by_expert(ap):
                return ap[:, :].rearrange("p (n s) -> p n s", n=N_EXP)

            def by_slot(ap):
                return ap[:, :].rearrange("p (n s) -> p s n", n=N_EXP)

            def front(q):
                a = q % 2
                if q == 0:
                    dve.wait_ge(bias_in, 16)
                wait(dve, dsub_pool, q - 1)
                for c in range(LC):
                    n = LC * q + c
                    dve.wait_ge(logit_pe, n + 1)
                    cols = slice(512 * c, 512 * c + 512)
                    v.tensor_tensor(logit[a][:, cols], turned[0:PT, n % 2, :], bias_bc[:, cols],
                                    ALU.add).then_inc(logit_dve, 1)
                dve.wait_ge(logit_dve, LC * (q + 1))
                v.tensor_reduce(dmax[a][:, :], by_expert(logit[a]), AX.X, ALU.max).then_inc(dmax_dve, 1)
                v.tensor_reduce(cmax[a][:, :], by_slot(logit[a]), AX.X, ALU.max).then_inc(cmax_dve, 1)
                dve.wait_ge(cmax_dve, q + 1)
                wait(dve, combT_pe, NS // 4 * (q - 1))
                v.tensor_tensor(by_expert(comb[a]), by_expert(logit[a]),
                                cmax[a][:, :].unsqueeze(1).broadcast_to([PT, N_EXP, P_SLOT]),
                                ALU.subtract).then_inc(csub_dve, 1)

            def back(q):
                a = q % 2
                dve.wait_ge(dexp_act, q + 1)
                v.tensor_reduce(dsum[a][:, :], by_expert(disp[a]), AX.X, ALU.add).then_inc(dsum_dve, 1)
                dve.wait_ge(dsum_dve, q + 1)
                v.reciprocal(dsum[a][:, :], dsum[a][:, :]).then_inc(drec_dve, 1)
                dve.wait_ge(cexp_act, q + 1)
                v.tensor_reduce(csum[a][:, :], by_slot(comb[a]), AX.X, ALU.add).then_inc(csum_dve, 1)
                dve.wait_ge(csum_dve, q + 1)
                v.reciprocal(csum[a][:, :], csum[a][:, :]).then_inc(crec_dve, 1)

            front(0)
            for q in range(NQ):
                if q + 1 < NQ:
                    front(q + 1)
                back(q)

            dve.wait_ge(xt_pe, NQ)
            for r, k in enumerate((0, 1, 2, 5)):
                v.tensor_scalar(xt[:, 4 * r:4 * r + 4, :], heads4(bank(k), 128), -33000.0, 65000.0,
                                ALU.max, ALU.min).then_inc(clip_dve, 1)
            for k in range(NS):
                dve.wait_ge(clip_dve, k // 4 + 1)
                s = v.bn_stats(xt_st[:, k, :], xt[:, k, :])
            s.then_inc(stat_dve, 1)
            dve.wait_ge(stat_dve, 1)
            for k in range(NS):
                s = v.bn_aggr(xt_mv[:, k, :], xt_st[:, k, :])
            s.then_inc(stat_dve, 1)
            dve.wait_ge(stat_dve, 2)
            v.tensor_scalar_add(xt_std[:, :], xt_mv[:, :, 1], EPS).then_inc(stat_dve, 1)
            dve.wait_ge(std_ready, 3)
            v.reciprocal(xt_rs[:, :], xt_std[:, :]).then_inc(stat_dve, 1)
            dve.wait_ge(stat_dve, 4)
            for k in range(NS):
                v.tensor_scalar(xt[:, k, :], xt[:, k, :], xt_mv[:, k, 0:1], xt_rs[:, k:k + 1],
                                ALU.subtract, ALU.mult).then_inc(norm_dve, 1)
            dve.wait_ge(eb_in, 16 * EPT)
            for r, k in enumerate((0, 1, 2, 5)):
                dve.wait_ge(yt_pe, r + 1)
                v.tensor_tensor(yt[:, 4 * r:4 * r + 4, :], heads4(bank(k), 128), eb[:, 4 * r:4 * r + 4, :],
                                ALU.add).then_inc(yt_dve, 1)
            dve.wait_ge(y2turn_pe, 1)
            v.tensor_tensor(out_sb[:, :, :], x1[:, :, :], misc[0:PT, 0, :].rearrange("p (q d) -> p q d", q=NQ),
                            ALU.add).then_inc(out_dve, 1)


_INS = ['x', 'ctx_1024', 'L0_xattn_Wq', 'L0_xattn_Wk', 'L0_xattn_Wv', 'L0_xattn_Wo',
        'L0_ffn_phi_w', 'L0_ffn_phi_b', 'L0_ffn_expert_w', 'L0_ffn_expert_b']
_OUTS = [((8, 56, 128), 'float32')]


def kernel(**inputs):
    import numpy as _np
    import concourse.bacc as _bacc
    from concourse import mybir as _mybir
    from concourse.bass_utils import run_bass_kernel_spmd as _run

    nc = _bacc.Bacc("TRN2", target_bir_lowering=False, num_devices=1)
    arrays, args = {}, []
    for name in _INS:
        a = _np.ascontiguousarray(inputs[name])
        arrays[f"in_{name}_dram"] = a
        args.append(nc.dram_tensor(f"in_{name}_dram", a.shape, _mybir.dt.from_np(a.dtype), kind="ExternalInput").ap())
    for i, (shape, dtype) in enumerate(_OUTS):
        dt = _mybir.dt.from_np(_np.dtype(dtype))
        args.append(nc.dram_tensor(f"out_{i}_dram", shape, dt, kind="ExternalOutput").ap())
    xattn_softmoe_kernel(nc, *args)
    r = _run(nc, [arrays], core_ids=[0])
    got = tuple(r.results[0][f"out_{i}_dram"] for i in range(len(_OUTS)))
    return got[0]
```

```python
from contextlib import ExitStack

import concourse.bass as bass
from concourse import mybir

F32 = mybir.dt.float32
F32R = mybir.dt.float32r
ALU = mybir.AluOpType
ACT = mybir.ActivationFunctionType
AX = mybir.AxisListType


def xattn_softmoe_kernel(
    nc: bass.Bass,
    x: bass.AP,
    ctx_1024: bass.AP,
    Wq: bass.AP,
    Wk: bass.AP,
    Wv: bass.AP,
    Wo: bass.AP,
    phi_w: bass.AP,
    phi_b: bass.AP,
    expert_w: bass.AP,
    expert_b: bass.AP,
    out: bass.AP,
):
    B, T, D = x.shape
    M = ctx_1024.shape[1]
    INNER = Wq.shape[1]
    DH = 64
    HEADS = INNER // DH
    ROWS = HEADS * T
    NT = ROWS // 128
    NC = 12
    CK = M // NC
    KB = 3
    KW = M // KB
    CPB = NC // KB
    PAIRS = B // 2
    PT = 2 * T
    TOK = B * T
    EPS = 1e-5
    SCALE = DH ** -0.5
    N_EXP, _, H = expert_w.shape
    SLOTS = phi_w.shape[0]
    P_SLOT = SLOTS // N_EXP
    NS = SLOTS // 128
    EPT = 128 // P_SLOT
    NQ = TOK // PT
    LC = SLOTS // 512
    assert ROWS == NT * 128 and NT == 7 and M == NC * CK and KW <= 512 and D == 128
    GROUPS = ((0, 3), (3, 7))

    def wait(eng, sem, value):
        if isinstance(value, int) and value <= 0:
            return
        eng.wait_ge(sem, value)

    with ExitStack() as ctx:
        def sem(name):
            return ctx.enter_context(nc.semaphore(name))

        def sb(name, shape, dt=F32):
            return ctx.enter_context(nc.sbuf_tensor(name, shape, dt))

        scores = ctx.enter_context(nc.psum_tensor("scores", [128, KB, 512], F32))
        turned = ctx.enter_context(nc.psum_tensor("turned", [128, 2, 512], F32))
        acc = ctx.enter_context(nc.psum_tensor("acc", [128, 512], F32))
        misc = ctx.enter_context(nc.psum_tensor("misc", [128, 2, 512], F32))

        ident = sb("ident", [128, 128])
        zero = sb("zero", [128, 1])
        neghalf = sb("neghalf", [128, NQ])
        x_sb = sb("x_sb", [PT, NQ, D])
        yT = sb("yT", [D, TOK])
        xnT = sb("xnT", [D, TOK])
        phiT = sb("phiT", [D, SLOTS])
        lnbuf = sb("lnbuf", [PT, NQ, 6])
        lnmv = sb("lnmv", [PT, NQ, 2])
        lnvar = sb("lnvar", [PT, NQ])
        lnrs = sb("lnrs", [PT, NQ])

        place = [(nc.sbuf_base + 63) // 64 * 64]

        def at(name, shape, dt, address):
            return nc.alloc_sbuf_tensor_at(name, shape, dt, offset=address)

        def nbytes(shape):
            n = 4
            for d in shape[1:]:
                n *= d
            return n

        def take(name, shape, dt=F32):
            address = place[0]
            place[0] += (nbytes(shape) + 31) // 32 * 32
            return at(name, shape, dt, address), address

        pT_h, pT_h_at = take("pT_h", [128, NT, NC, 128], F32R)
        pT_l, pT_l_at = take("pT_l", [128, NT, NC, 128], F32R)
        TILE = nbytes([1, NC, 128])
        prob0, prob_at = take("prob0", [128, M])
        prob = [prob0, take("prob1", [128, M])[0]]
        ctx_raw, ctx_raw_at = take("ctx_raw", [CK, NC, D])
        ctx_nh0, n0_at = take("ctx_nh0", [CK, NC, D], F32R)
        ctx_nl0, _ = take("ctx_nl0", [CK, NC, D], F32R)
        ctx_th0, t0_at = take("ctx_th0", [D, M], F32R)
        ctx_tl0, _ = take("ctx_tl0", [D, M], F32R)
        ctx_nh1, n1_at = take("ctx_nh1", [CK, NC, D], F32R)
        ctx_nl1, _ = take("ctx_nl1", [CK, NC, D], F32R)
        ctx_th1, t1_at = take("ctx_th1", [D, M], F32R)
        ctx_tl1, _ = take("ctx_tl1", [D, M], F32R)
        ctx_nh, ctx_nl, ctx_th, ctx_tl = [ctx_nh0, ctx_nh1], [ctx_nl0, ctx_nl1], [ctx_th0, ctx_th1], [ctx_tl0, ctx_tl1]
        qk_h0, qk_at = take("qk_h0", [D, HEADS, T], F32R)
        qk_l0, _ = take("qk_l0", [D, HEADS, T], F32R)
        qk_h1, _ = take("qk_h1", [D, HEADS, T], F32R)
        qk_l1, _ = take("qk_l1", [D, HEADS, T], F32R)
        qk_h, qk_l = [qk_h0, qk_h1], [qk_l0, qk_l1]
        qk_raw, _ = take("qk_raw", [D, HEADS, T])
        wqk, wqk_at = take("wqk", [D, HEADS, D])
        wvo, _ = take("wvo", [D, HEADS, D])
        oT, oT_at = take("oT", [D, 2, HEADS, T])
        oT_cols = oT[:, :, :, :].rearrange("p b h t -> p b (h t)")
        rbc, rbc_at = take("rbc", [128, 512])
        bankmax, _ = take("bankmax", [128, 2, KB])
        negmax, _ = take("negmax", [128, 2])
        den, _ = take("den", [128, 2 * NT])
        rden, _ = take("rden", [128, 2 * NT])
        assert place[0] <= nc.sbuf_usable_end

        KB4 = 4096
        wq_sb = at("wq_sb", [D, INNER], F32, pT_h_at)
        wk_sb = at("wk_sb", [D, INNER], F32, pT_h_at + KB4)
        wqT = at("wqT", [128, HEADS // 2, D], F32, pT_h_at + 2 * KB4)
        wkT = at("wkT", [128, HEADS // 2, D], F32, pT_h_at + 3 * KB4)
        xn = at("xn", [PT, NQ, D], F32, pT_h_at + 4 * KB4)
        wv_sb = at("wv_sb", [D, INNER], F32, pT_h_at + 3 * TILE)
        wo_sb = at("wo_sb", [128, HEADS // 2, D], F32, pT_h_at + 3 * TILE + KB4)
        wvT = at("wvT", [128, HEADS // 2, D], F32, pT_h_at + 3 * TILE + 2 * KB4)

        KB8 = 8192
        logit = [at("logit0", [PT, SLOTS], F32, pT_h_at), at("logit1", [PT, SLOTS], F32, pT_h_at + KB8),
                 at("logit2", [PT, SLOTS], F32, t1_at), at("logit3", [PT, SLOTS], F32, qk_at)]
        disp = [at("disp0", [PT, SLOTS], F32, pT_l_at + 2048), at("disp1", [PT, SLOTS], F32, pT_l_at + 2048 + KB8),
                at("disp2", [PT, SLOTS], F32, wqk_at), at("disp3", [PT, SLOTS], F32, qk_at + KB8)]
        comb = logit
        x1 = at("x1", [PT, NQ, D], F32, ctx_raw_at)
        x2n = at("x2n", [PT, NQ, D], F32, ctx_raw_at + 2048)
        x2nT = at("x2nT", [D, TOK], F32, ctx_raw_at + 4096)
        b_raw = at("b_raw", [128, 512], F32, n0_at)
        b_h = at("b_h", [128, 512], F32R, n0_at + 2048)
        b_l = at("b_l", [128, 512], F32R, n0_at + 4096)
        pick = at("pick", [128, LC, PT], F32, n0_at + 6144)
        pick_r = at("pick_r", [128, LC, PT], F32R, n0_at + 8192)
        phi_sb = at("phi_sb", [128, NS, D], F32, t0_at)
        dmax = [at(f"dmax{q}", [PT, N_EXP], F32, t0_at + KB8 + 256 * q) for q in range(NQ)]
        dsum = [at(f"dsum{q}", [PT, N_EXP], F32, t0_at + KB8 + 1024 + 256 * q) for q in range(NQ)]
        cmax = [at(f"cmax{q}", [PT, P_SLOT], F32, t0_at + KB8 + 2048 + 128 * q) for q in range(NQ)]
        csum = [at(f"csum{q}", [PT, P_SLOT], F32, t0_at + KB8 + 2560 + 128 * q) for q in range(NQ)]
        combT = at("combT", [128, NS, TOK], F32, pT_h_at + 2 * KB8)
        ew = at("ew", [D, N_EXP, H], F32, pT_l_at + 3 * TILE)
        eb = at("eb", [128, NS, H], F32, n1_at)
        xt = at("xt", [128, NS, D], F32, pT_l_at + 2048)
        xtT = at("xtT", [128, NS, 128], F32, pT_l_at + 2048 + KB8)
        yt = at("yt", [128, NS, H], F32, wqk_at)
        y2T = at("y2T", [H, TOK], F32, oT_at)
        out_sb = at("out_sb", [PT, NQ, D], F32, oT_at + 2048)
        xt_st = at("xt_st", [128, NS, 6], F32, rbc_at)
        xt_mv = at("xt_mv", [128, NS, 2], F32, rbc_at + 384)
        xt_var = at("xt_var", [128, NS], F32, rbc_at + 512)
        xt_rs = at("xt_rs", [128, NS], F32, rbc_at + 576)
        xt_nb = at("xt_nb", [128, NS], F32, rbc_at + 640)

        x_in = sem("x_in")
        wq_in = sem("wq_in")
        wk_in = sem("wk_in")
        wvo_in = sem("wvo_in")
        zeroed = sem("zeroed")
        ident_ready = sem("ident_ready")
        ln_stat = sem("ln_stat")
        ln_mv = sem("ln_mv")
        ln_var = sem("ln_var")
        ln_std = sem("ln_std")
        ln_rs = sem("ln_rs")
        xn_ready = sem("xn_ready")
        setup_pe = sem("setup_pe")
        setup_act = sem("setup_act")
        setup_dve = sem("setup_dve")
        ctx0_in = [sem(f"ctx0_in{k}") for k in range(KB)]
        ctx_in = sem("ctx_in")
        ctx_nat = sem("ctx_nat")
        nat_hi = sem("nat_hi")
        ctxT_pe = sem("ctxT_pe")
        ctxT_hi = sem("ctxT_hi")
        ctxT_lo = sem("ctxT_lo")
        qk_pe = sem("qk_pe")
        qk_hi = sem("qk_hi")
        qk_lo = sem("qk_lo")
        qkb_hi = sem("qkb_hi")
        qkb_lo = sem("qkb_lo")
        scores_pe = sem("scores_pe")
        bmax_dve = sem("bmax_dve")
        negmax_dve = sem("negmax_dve")
        exp_act = sem("exp_act")
        turned_pe = sem("turned_pe")
        pT_hi = sem("pT_hi")
        pT_lo = sem("pT_lo")
        pv_pe = sem("pv_pe")
        rden_dve = sem("rden_dve")
        rbc_pe = sem("rbc_pe")
        rbc_act = sem("rbc_act")
        oT_dve = sem("oT_dve")
        y_pe = sem("y_pe")
        y_act = sem("y_act")
        bias_in = sem("bias_in")
        phi_in = sem("phi_in")
        ew_in = sem("ew_in")
        eb_in = sem("eb_in")
        bias_zero = sem("bias_zero")
        pick_ready = sem("pick_ready")
        bias_hi = sem("bias_hi")
        bias_lo = sem("bias_lo")
        phi_pe = sem("phi_pe")
        phi_cp = sem("phi_cp")
        yturn_pe = sem("yturn_pe")
        x1_dve = sem("x1_dve")
        x2n_dve = sem("x2n_dve")
        x2nT_pe = sem("x2nT_pe")
        x2nT_act = sem("x2nT_act")
        logit_pe = sem("logit_pe")
        logit_act = sem("logit_act")
        dmax_dve = sem("dmax_dve")
        cmax_dve = sem("cmax_dve")
        dsub_pool = sem("dsub_pool")
        csub_dve = sem("csub_dve")
        dexp_act = sem("dexp_act")
        cexp_act = sem("cexp_act")
        dsum_dve = sem("dsum_dve")
        csum_dve = sem("csum_dve")
        drec_dve = sem("drec_dve")
        crec_dve = sem("crec_dve")
        disp_pool = sem("disp_pool")
        comb_pool = sem("comb_pool")
        xt_pe = sem("xt_pe")
        combT_pe = sem("combT_pe")
        combT_act = sem("combT_act")
        clip_dve = sem("clip_dve")
        stat_dve = sem("stat_dve")
        mv_dve = sem("mv_dve")
        var_dve = sem("var_dve")
        rs_pool = sem("rs_pool")
        nb_dve = sem("nb_dve")
        tanh_act = sem("tanh_act")
        xtT_pe = sem("xtT_pe")
        xtT_act = sem("xtT_act")
        yt_pe = sem("yt_pe")
        yt_dve = sem("yt_dve")
        y2_pe = sem("y2_pe")
        y2_act = sem("y2_act")
        y2turn_pe = sem("y2turn_pe")
        out_dve = sem("out_dve")
        stored = sem("stored")

        ctx_v = ctx_1024.rearrange("b (p j) d -> b p j d", j=NC)
        x_v = x.rearrange("(q b) t d -> (b t) q d", b=2)
        out_v = out.rearrange("(q b) t d -> (b t) q d", b=2)

        S0, S1, S2, T0, T1, ACC, M0, M1 = range(8)

        def bank(k):
            return [scores[:, 0, :], scores[:, 1, :], scores[:, 2, :], turned[:, 0, :],
                    turned[:, 1, :], acc[:, :], misc[:, 0, :], misc[:, 1, :]][k]

        RING = (T0, T1, S1, S2)
        SLOT_BANKS = (S0, ACC, M0, M1)

        def blocks4(ap, w=128):
            return ap[:, 0:4 * w].rearrange("p (h c) -> p h c", h=4)

        def rounds_of_qk(t):
            return min(4, -(-(-(-128 * (t + 1) // T)) // 4))

        LAST = PAIRS - 1
        block = ctx.enter_context(nc.Block())

        @block.sync
        def _(sp):
            sp.dma_start(x_sb[:, :, :], x_v).then_inc(x_in, 16)
            for k in range(KB):
                chunks = slice(CPB * k, CPB * k + CPB)
                sp.dma_start(ctx_raw[:, chunks, :], ctx_v[0][:, chunks, :]).then_inc(ctx0_in[k], 16)

            def load_ctx(b):
                sp.wait_ge(ctxT_pe, KB * b)
                sp.wait_ge(ctx_nat, b)
                sp.dma_start(ctx_raw[:, :, :], ctx_v[b]).then_inc(ctx_in, 16)

            load_ctx(1)
            with sp.Fori(1, PAIRS) as i:
                load_ctx(2 * i)
                load_ctx(2 * i + 1)

            sp.wait_ge(scores_pe, KB * NT * (B - 1))
            sp.dma_start(phi_sb[:, :, :], phi_w.rearrange("(k p) d -> p k d", p=128)).then_inc(phi_in, 16)
            sp.wait_ge(bias_zero, 2)
            sp.dma_start(b_raw[0:LC, :], phi_b.rearrange("(c e) -> c e", c=LC)).then_inc(bias_in, 16)
            sp.wait_ge(pv_pe, 2 * B)
            sp.dma_start(ew[:, :, :], expert_w.rearrange("n d h -> d n h")).then_inc(ew_in, 16)
            eb_v = expert_b.rearrange("(k n) h -> n k h", n=EPT)
            for n in range(EPT):
                sp.dma_start(eb[n * P_SLOT:(n + 1) * P_SLOT, :, :],
                             eb_v[n].partition_broadcast(P_SLOT)).then_inc(eb_in, 16)
            sp.wait_ge(out_dve, 1)
            sp.dma_start(out_v, out_sb[:, :, :]).then_inc(stored, 16)
            sp.wait_ge(stored, 16)

        @block.gpsimd
        def _(pool):
            gp = nc.gpsimd
            gp.memset(ident[:, :], 0.0).then_inc(zeroed, 1)
            gp.memset(zero[:, :], 0.0).then_inc(zeroed, 1)
            gp.memset(neghalf[:, :], -0.5).then_inc(zeroed, 1)
            pool.wait_ge(zeroed, 3)
            gp.affine_select(out=ident[:, :], in_=ident[:, :], compare_op=ALU.not_equal,
                             fill=1.0, base=0, pattern=[[-1, 128]],
                             channel_multiplier=1).then_inc(ident_ready, 1)

            def split_ctx(b, a, first=False):
                if first:
                    for k in range(KB):
                        pool.wait_ge(ctx0_in[k], 16)
                else:
                    pool.wait_ge(ctx_in, 16 * b)
                wait(pool, pv_pe, 2 * (b - 1))
                gp.tensor_tensor(ctx_nh[a][:, :, :].rearrange("p j d -> p (j d)"),
                                 ctx_raw[:, :, :].rearrange("p j d -> p (j d)"),
                                 zero[0:CK, :].broadcast_to([CK, NC * D]), ALU.add).then_inc(nat_hi, 1)
                pool.wait_ge(nat_hi, b + 1)
                gp.tensor_tensor(ctx_nl[a][:, :, :], ctx_raw[:, :, :],
                                 ctx_nh[a][:, :, :].bitcast(F32), ALU.subtract).then_inc(ctx_nat, 1)

            def split_qk(i):
                pool.wait_ge(qk_lo, 4 * (i + 1))
                wait(pool, scores_pe, KB * 2 * NT * i)
                gp.tensor_tensor(qk_h[1][:, :, :].rearrange("p h t -> p (h t)"),
                                 qk_raw[:, :, :].rearrange("p h t -> p (h t)"),
                                 zero[:, :].broadcast_to([D, ROWS]), ALU.add).then_inc(qkb_hi, 1)
                pool.wait_ge(qkb_hi, i + 1)
                gp.tensor_tensor(qk_l[1][:, :, :], qk_raw[:, :, :],
                                 qk_h[1][:, :, :].bitcast(F32), ALU.subtract).then_inc(qkb_lo, 1)

            def pair(i, last=False):
                split_qk(i)
                split_ctx(2 * i + 1, 1)
                if not last:
                    split_ctx(2 * i + 2, 0)

            split_ctx(0, 0, first=True)
            pair(0)
            with pool.Fori(1, LAST) as i:
                pair(i)
            pair(LAST, last=True)

            pool.wait_ge(pv_pe, 2 * (B - 1))
            gp.memset(b_raw[:, :], 0.0).then_inc(bias_zero, 1)
            gp.memset(pick[:, :, :], 0.0).then_inc(bias_zero, 1)
            pool.wait_ge(bias_zero, 2)
            gp.affine_select(out=pick[:, :, :], in_=pick[:, :, :], compare_op=ALU.not_equal, fill=1.0,
                             base=0, pattern=[[-1, LC], [0, PT]],
                             channel_multiplier=1).then_inc(bias_zero, 1)
            pool.wait_ge(bias_zero, 3)
            gp.tensor_copy(pick_r[:, :, :], pick[:, :, :]).then_inc(pick_ready, 1)
            pool.wait_ge(bias_in, 16)
            gp.tensor_copy(b_h[:, :], b_raw[:, :]).then_inc(bias_hi, 1)
            pool.wait_ge(bias_hi, 1)
            gp.tensor_tensor(b_l[:, :], b_raw[:, :], b_h[:, :].bitcast(F32), ALU.subtract).then_inc(bias_lo, 1)

            def root(n, q0, q1):
                pool.wait_ge(ln_var, n + 1)
                gp.tensor_tensor(lnrs[:, q0:q1], lnvar[:, q0:q1], neghalf[0:PT, q0:q1],
                                 ALU.pow).then_inc(ln_rs, 1)

            def by_expert(ap):
                return ap[:, :].rearrange("p (n s) -> p n s", n=N_EXP)

            def dispatch_shift(q):
                pool.wait_ge(dmax_dve, q + 1)
                gp.tensor_tensor(by_expert(disp[q]), by_expert(logit[q]),
                                 dmax[q][:, :].unsqueeze(2).broadcast_to([PT, N_EXP, P_SLOT]),
                                 ALU.subtract).then_inc(dsub_pool, 1)

            def dispatch_scale(q):
                pool.wait_ge(drec_dve, q + 1)
                gp.tensor_tensor(by_expert(disp[q]), by_expert(disp[q]),
                                 dsum[q][:, :].unsqueeze(2).broadcast_to([PT, N_EXP, P_SLOT]),
                                 ALU.mult).then_inc(disp_pool, 1)

            def combine_scale(q):
                pool.wait_ge(crec_dve, q + 1)
                gp.tensor_tensor(by_expert(comb[q]), by_expert(comb[q]),
                                 csum[q][:, :].unsqueeze(1).broadcast_to([PT, N_EXP, P_SLOT]),
                                 ALU.mult).then_inc(comb_pool, 1)

            root(1, 0, LAST)
            dispatch_shift(0)
            dispatch_scale(0)
            root(2, LAST, NQ)
            for q in range(1, NQ):
                dispatch_shift(q)
                if q < LAST:
                    combine_scale(q - 1)
                dispatch_scale(q)
            combine_scale(LAST - 1)
            combine_scale(LAST)
            for r in range(4):
                pool.wait_ge(var_dve, r + 1)
                gp.tensor_tensor(xt_rs[:, 4 * r:4 * r + 4], xt_var[:, 4 * r:4 * r + 4], neghalf[:, 0:4],
                                 ALU.pow).then_inc(rs_pool, 1)

        @block.tensor
        def _(pe):
            mm = nc.tensor.matmul
            tr = nc.tensor.transpose

            def turn_ctx(b, k, m, first=False):
                if first:
                    pe.wait_ge(ctx0_in[k], 16)
                else:
                    pe.wait_ge(ctx_in, 16 * b)
                for c in range(CPB):
                    last = tr(misc[:, m, CK * c:CK * c + CK], ctx_raw[:, CPB * k + c, :], ident[0:CK, 0:CK])
                last.then_inc(ctxT_pe, 1)

            def make_qk(i, r, m):
                for c in range(4):
                    last = mm(misc[:, m, PT * c:PT * c + PT], wqk[:, 4 * r + c, :],
                              xnT[:, bass.ds(i * PT, PT)], start=True, stop=True)
                last.then_inc(qk_pe, 1)

            def turn_weight(w, half, k):
                for c in range(4):
                    j = 4 * half + c
                    last = tr(bank(k)[:, 128 * c:128 * c + 128], w[:, 128 * j:128 * j + 128], ident[:, :])
                last.then_inc(setup_pe, 1)

            def head_products(wT, right, r, k):
                p = DH * (r % 2)
                for c in range(4):
                    j = r // 2 * 4 + c
                    last = mm(bank(k)[:, 128 * c:128 * c + 128], wT[p:p + DH, j, :],
                              right[p:p + DH, j, :], start=True, stop=True)
                last.then_inc(setup_pe, 1)

            pe.wait_ge(ident_ready, 1)
            pe.wait_ge(xn_ready, 1)
            for q in range(NQ):
                last = tr(bank(ACC)[:, PT * q:PT * q + PT], xn[:, q, :], ident[0:PT, 0:PT])
            last.then_inc(setup_pe, 1)
            turn_ctx(0, 0, 1, first=True)
            turn_ctx(0, 1, 0, first=True)
            pe.wait_ge(ctxT_lo, 1)
            turn_ctx(0, 2, 1, first=True)
            pe.wait_ge(wq_in, 16)
            turn_weight(wq_sb, 0, S0)
            turn_weight(wq_sb, 1, S1)
            pe.wait_ge(wk_in, 16)
            turn_weight(wk_sb, 0, S2)
            turn_weight(wk_sb, 1, T0)
            pe.wait_ge(setup_dve, 3)
            head_products(wqT, wkT, 0, T1)
            head_products(wqT, wkT, 1, ACC)
            pe.wait_ge(setup_act, 2)
            head_products(wqT, wkT, 2, S0)
            head_products(wqT, wkT, 3, S1)
            pe.wait_ge(setup_act, 3)
            pe.wait_ge(setup_dve, 4)
            pe.wait_ge(ctxT_lo, 3)
            make_qk(0, 0, 0)
            make_qk(0, 1, 1)

            def make_scores(g, a, t):
                wait(pe, exp_act, g)
                rows = slice(128 * t, 128 * t + 128)
                hi = qk_h[a][:, :, :].rearrange("p h t -> p (h t)")[:, rows]
                lo = qk_l[a][:, :, :].rearrange("p h t -> p (h t)")[:, rows]
                for k in range(KB):
                    o = scores[:, k, 0:KW]
                    keys = slice(KW * k, KW * k + KW)
                    mm(o, hi, ctx_th[a][:, keys], start=True, stop=False)
                    mm(o, hi, ctx_tl[a][:, keys], start=False, stop=False)
                    mm(o, lo, ctx_th[a][:, keys], start=False, stop=True).then_inc(scores_pe, 1)

            def turn_probs(g, u, k):
                m = (KB * u + k) % 2
                wait(pe, pT_lo, KB * g + k - 1)
                if k == 0:
                    pe.wait_ge(exp_act, g + 1)
                for c in range(CPB):
                    j = CPB * k + c
                    last = tr(turned[0:CK, m, 128 * c:128 * c + 128], prob[u][:, CK * j:CK * j + CK],
                              ident[:, :])
                last.then_inc(turned_pe, 1)

            def context_product(b, a, grp, chunks):
                t0, t1 = GROUPS[grp]
                o = acc[:, 0:128 * (t1 - t0)].rearrange("p (t r) -> p t r", r=128)
                if chunks[0] == 0:
                    pe.wait_ge(pT_lo, KB * (b * NT + t1))
                    pe.wait_ge(ctx_nat, b + 1)
                    wait(pe, oT_dve, b * 2 + grp)
                for j in chunks:
                    hi, lo = pT_h[0:CK, t0:t1, j, :], pT_l[0:CK, t0:t1, j, :]
                    mm(o, ctx_nh[a][:, j, :], hi, start=(j == 0), stop=False)
                    mm(o, ctx_nh[a][:, j, :], lo, start=False, stop=False)
                    last = mm(o, ctx_nl[a][:, j, :], hi, start=False, stop=(j == NC - 1))
                if chunks[-1] == NC - 1:
                    last.then_inc(pv_pe, 1)

            def spread_rden(a, grp, m):
                t0, t1 = GROUPS[grp]
                for t in range(t0, t1):
                    last = tr(misc[:, m, 128 * (t - t0):128 * (t - t0) + 128],
                              rden[:, a * NT + t:a * NT + t + 1].broadcast_to([128, 128]), ident[:, :])
                last.then_inc(rbc_pe, 1)

            def project(r):
                for h in range(8 * r, 8 * r + 8):
                    last = mm(misc[:, 0, 0:PT].rearrange("p (b t) -> p b t", b=2), wvo[:, h, :],
                              oT[:, :, h, :], start=(h == 0), stop=(h == HEADS - 1))
                return last

            def half(i, a, first=False, last=False):
                b = i * 2 + a
                for t in range(NT):
                    g = b * NT + t
                    before = not (first and t == 0)
                    u = (a + t + 1) % 2
                    if t == 0:
                        pe.wait_ge(ctxT_lo, KB * (b + 1))
                        if a == 1:
                            pe.wait_ge(qkb_lo, i + 1)
                    if a == 0:
                        pe.wait_ge(qk_lo, i * 4 + rounds_of_qk(t))
                    make_scores(g, a, t)
                    if before:
                        turn_probs(g - 1, u, 0)
                        turn_probs(g - 1, u, 1)
                    if 1 <= t <= 3 and not first:
                        share = (b - 1, 1 - a, 1, range(4 * t - 4, 4 * t))
                    elif t >= 4 and last:
                        share = (b, a, 0, range(4 * t - 16, 4 * t - 12))
                    elif t >= 4:
                        share = (b, a, 0, range(3 * t - 12, 3 * t - 9))
                    elif t == 0 and not first:
                        share = (b - 1, 1 - a, 0, range(9, NC))
                    else:
                        share = None
                    if first and t == 4:
                        pe.wait_ge(setup_act, 7)
                    if share:
                        context_product(*share[0:3], share[3][0:-1])
                    if before:
                        turn_probs(g - 1, u, 2)
                    if share:
                        context_product(*share[0:3], share[3][-1:])
                    if first:
                        if t == 0:
                            pe.wait_ge(wvo_in, 32)
                            turn_weight(wv_sb, 0, ACC)
                            pe.wait_ge(setup_act, 4)
                            pe.wait_ge(setup_dve, 5)
                            pe.wait_ge(qk_lo, 1)
                            make_qk(0, 2, 0)
                        if t == 1:
                            pe.wait_ge(setup_act, 5)
                            turn_weight(wv_sb, 1, ACC)
                            pe.wait_ge(qk_lo, 2)
                            make_qk(0, 3, 1)
                        if t == 2:
                            pe.wait_ge(setup_dve, 6)
                            head_products(wvT, wo_sb, 0, ACC)
                            pe.wait_ge(qk_lo, 3)
                            head_products(wvT, wo_sb, 2, M0)
                            pe.wait_ge(qk_lo, 4)
                            turn_ctx(1, 0, 1)
                        if t == 3:
                            pe.wait_ge(setup_act, 6)
                            head_products(wvT, wo_sb, 1, ACC)
                            pe.wait_ge(setup_dve, 7)
                            turn_ctx(1, 1, 0)
                            pe.wait_ge(ctxT_lo, KB + 1)
                            head_products(wvT, wo_sb, 3, M1)
                        if t == 4:
                            pe.wait_ge(setup_dve, 8)
                            turn_ctx(1, 2, 1)
                    if a == 1 and t == 0 and not last:
                        wait(pe, y_act, i)
                        pe.wait_ge(ctxT_lo, KB * b + 2)
                        make_qk(i + 1, 0, 0)
                    if t == 1 and not first:
                        pe.wait_ge(rden_dve, b * 2)
                        pe.wait_ge(rbc_act, b * 2 - 1)
                        spread_rden(1 - a, 1, a)
                    if 2 <= t <= 4 and not last and not first:
                        k = t - 2
                        if k == 2:
                            pe.wait_ge(ctxT_lo, KB * (b + 1) + 1)
                        elif k == 1:
                            wait(pe, rbc_act, b * 2)
                        elif a == 0:
                            pe.wait_ge(qk_lo, (i + 1) * 4)
                        else:
                            pe.wait_ge(qk_lo, (i + 1) * 4 + 1)
                        turn_ctx(b + 1, k, (1 + k + a) % 2)
                    if a == 1 and 4 <= t <= 6 and not last:
                        if t < 6:
                            pe.wait_ge(ctxT_lo, KB * (b + 1) + (t - 2))
                        else:
                            pe.wait_ge(qk_lo, (i + 1) * 4 + 2)
                        make_qk(i + 1, t - 3, (t - 3) % 2)
                    if a == 0 and t == 5 and not first:
                        pe.wait_ge(oT_dve, b * 2)
                        pe.wait_ge(ctxT_lo, KB * (b + 1) + 2)
                        project(0)
                    if t == 6:
                        if a == 0 and not first:
                            project(1).then_inc(y_pe, 1)
                        pe.wait_ge(rden_dve, b * 2 + 1)
                        if a == 0:
                            pe.wait_ge(ctxT_lo, KB * (b + 1) + 3)
                        elif not last:
                            pe.wait_ge(qk_lo, (i + 1) * 4 + 3)
                        else:
                            pe.wait_ge(y_act, i)
                        spread_rden(a, 0, 1 - a)

            half(0, 0, first=True)
            half(0, 1)
            with pe.Fori(1, LAST) as i:
                half(i, 0)
                half(i, 1)
            half(LAST, 0)
            half(LAST, 1, last=True)

            def turn_y(q0, q1, k):
                for q in range(q0, q1):
                    last = tr(bank(k)[0:PT, D * q:D * q + D], yT[:, PT * q:PT * q + PT], ident[:, :])
                last.then_inc(yturn_pe, 1)

            def turn_x2n(q0, q1, k):
                for q in range(q0, q1):
                    last = tr(bank(k)[:, PT * q:PT * q + PT], x2n[:, q, :], ident[0:PT, 0:PT])
                last.then_inc(x2nT_pe, 1)

            def logits(q, cs=range(LC)):
                for c in cs:
                    o = bank(RING[c])[0:PT, :]
                    mm(o, x2nT[:, PT * q:PT * q + PT], phiT[:, 512 * c:512 * c + 512], start=True, stop=False)
                    mm(o, pick_r[:, c, :], b_h[:, :], start=False, stop=False)
                    mm(o, pick_r[:, c, :], b_l[:, :], start=False, stop=True).then_inc(logit_pe, 1)

            G = B * NT
            turn_probs(G - 1, 1, 0)
            turn_probs(G - 1, 1, 1)
            turn_y(0, LAST, S0)
            pe.wait_ge(phi_in, 16)
            for c in range(8):
                last = tr(bank((S1, S2)[c // 4])[:, 128 * (c % 4):128 * (c % 4) + 128], phi_sb[:, c, :], ident[:, :])
                if c % 4 == 3:
                    last.then_inc(phi_pe, 1)
            turn_probs(G - 1, 1, 2)
            pe.wait_ge(rden_dve, 2 * B)
            pe.wait_ge(rbc_act, 2 * B - 1)
            spread_rden(1, 1, 1)
            for r in range(2):
                pe.wait_ge(phi_cp, r + 1)
                for c in range(8 + 4 * r, 12 + 4 * r):
                    last = tr(bank((S1, S2)[r])[:, 128 * (c % 4):128 * (c % 4) + 128], phi_sb[:, c, :], ident[:, :])
                last.then_inc(phi_pe, 1)
            context_product(B - 1, 1, 1, range(0, 4))
            pe.wait_ge(x2n_dve, 1)
            pe.wait_ge(rbc_act, 2 * B - 1)
            turn_x2n(0, LAST, M0)
            context_product(B - 1, 1, 1, range(4, 6))
            pe.wait_ge(x2nT_act, 1)
            pe.wait_ge(phi_cp, 4)
            pe.wait_ge(pT_lo, KB * G)
            pe.wait_ge(bias_lo, 1)
            logits(0)
            context_product(B - 1, 1, 1, range(6, NC))
            pe.wait_ge(logit_act, LC)
            logits(1)
            pe.wait_ge(oT_dve, 2 * B)
            project(0)
            project(1).then_inc(y_pe, 1)
            pe.wait_ge(y_act, PAIRS)
            pe.wait_ge(x1_dve, 1)
            turn_y(LAST, NQ, S0)
            pe.wait_ge(x2n_dve, 2)
            turn_x2n(LAST, NQ, M0)
            pe.wait_ge(x2nT_act, 2)
            pe.wait_ge(x1_dve, 2)

            def slots_in(q):
                pe.wait_ge(disp_pool, q + 1)
                for k in range(NS):
                    last = mm(bank(SLOT_BANKS[k // 4])[:, 128 * (k % 4):128 * (k % 4) + 128],
                              disp[q][:, 128 * k:128 * k + 128], x2n[:, q, :],
                              start=(q == 0 and k % 4 == 0), stop=(q == LAST),
                              skip_group_check=True)
                    if q == LAST and k % 4 == 3:
                        last.then_inc(xt_pe, 1)

            def turn_comb(q):
                pe.wait_ge(comb_pool, q + 1)
                for r in range(4):
                    n = 4 * q + r
                    if q == 0:
                        pe.wait_ge(logit_act, LC * 2 + r + 1)
                    elif q == 1:
                        pe.wait_ge(logit_act, LC * 3 + r + 1)
                    else:
                        pe.wait_ge(combT_act, n - 3)
                    for c in range(4):
                        k = 4 * r + c
                        last = tr(bank(RING[r])[:, PT * c:PT * c + PT], comb[q][:, 128 * k:128 * k + 128],
                                  ident[0:PT, 0:PT])
                    last.then_inc(combT_pe, 1)

            slots_in(0)
            pe.wait_ge(logit_act, 2 * LC)
            logits(2)
            slots_in(1)
            turn_comb(0)
            for c in range(LC):
                pe.wait_ge(combT_act, c + 1)
                logits(3, [c])
            slots_in(2)
            turn_comb(1)
            slots_in(3)

            def turn_xt(r):
                pe.wait_ge(tanh_act, 4 * r + 4)
                for c in range(4):
                    last = tr(bank(RING[r])[:, 128 * c:128 * c + 128], xt[:, 4 * r + c, :], ident[:, :])
                last.then_inc(xtT_pe, 1)

            def experts(r):
                pe.wait_ge(xtT_act, r + 1)
                for k in range(4 * r, 4 * r + 4):
                    for e in range(EPT):
                        p = slice(P_SLOT * e, P_SLOT * e + P_SLOT)
                        last = mm(bank(SLOT_BANKS[r])[p, 128 * (k % 4):128 * (k % 4) + 128],
                                  xtT[:, k, p], ew[:, EPT * k + e, :], start=True, stop=True)
                last.then_inc(yt_pe, 1)

            def combine(r):
                pe.wait_ge(yt_dve, r + 1)
                for k in range(4 * r, 4 * r + 4):
                    last = mm(bank(S0)[:, 0:TOK], yt[:, k, :], combT[:, k, :], start=(k == 0), stop=(k == NS - 1))
                return last

            turn_comb(2)
            turn_comb(3)
            pe.wait_ge(ew_in, 16)
            for r in range(4):
                pe.wait_ge(combT_act, 12 + r + 1)
                turn_xt(r)
                experts(r)
                if r >= 1:
                    combine(r - 1)
            combine(3).then_inc(y2_pe, 1)
            pe.wait_ge(y2_act, 1)
            for q in range(NQ):
                last = tr(bank(T0)[0:PT, D * q:D * q + D], y2T[:, PT * q:PT * q + PT], ident[:, :])
            last.then_inc(y2turn_pe, 1)

        @block.scalar
        def _(act):
            act.dma_start(wq_sb[:, :], Wq).then_inc(wq_in, 16)
            act.dma_start(wk_sb[:, :], Wk).then_inc(wk_in, 16)
            act.dma_start(wv_sb[:, :], Wv).then_inc(wvo_in, 16)
            act.dma_start(wo_sb[:, :, :], Wo.rearrange("(j p) n -> p j n", p=128)).then_inc(wvo_in, 16)
            act.wait_ge(ln_var, 1)
            nc.scalar.activation(lnvar[:, :], lnvar[:, :], ACT.Sqrt).then_inc(ln_std, 1)

            def copy_out(n, dst, k, scale=None):
                act.wait_ge(setup_pe, n)
                if scale:
                    return nc.scalar.mul(dst, blocks4(bank(k)), scale).then_inc(setup_act, 1)
                return nc.scalar.copy(dst, blocks4(bank(k))).then_inc(setup_act, 1)

            def hi_ctx(b, a, k, m):
                act.wait_ge(ctxT_pe, KB * b + (k + 1))
                nc.scalar.copy(ctx_th[a][:, KW * k:KW * k + KW], misc[:, m, 0:KW]).then_inc(ctxT_hi, 1)

            def hi_qk(i, r, m):
                act.wait_ge(qk_pe, i * 4 + (r + 1))
                if r == 0:
                    wait(act, qkb_lo, i)
                both = misc[:, m, 0:4 * PT].rearrange("p (h b t) -> p b h t", h=4, b=2)
                nc.scalar.copy(qk_raw[:, 4 * r:4 * r + 4, :], both[:, 1])
                nc.scalar.copy(qk_h[0][:, 4 * r:4 * r + 4, :], both[:, 0]).then_inc(qk_hi, 1)

            def hi_probs(g, u, t, k):
                act.wait_ge(turned_pe, KB * g + (k + 1))
                nc.scalar.copy(pT_h[0:CK, t, CPB * k:CPB * k + CPB, :],
                               turned[0:CK, (KB * u + k) % 2, :].rearrange("p (c r) -> p c r", c=CPB)
                               ).then_inc(pT_hi, 1)

            def exp_tile(g, u, a, t):
                act.wait_ge(negmax_dve, g + 1)
                nc.scalar.activation(prob[u][:, :].rearrange("p (k w) -> p k w", k=KB), scores[:, :, 0:KW],
                                     ACT.Exp, bias=negmax[:, u:u + 1],
                                     accum_out=den[:, a * NT + t:a * NT + t + 1]).then_inc(exp_act, 1)

            def copy_rbc(n, grp, m):
                act.wait_ge(rbc_pe, n)
                wait(act, oT_dve, n - 1)
                w = 128 * (GROUPS[grp][1] - GROUPS[grp][0])
                nc.scalar.copy(rbc[:, 0:w], misc[:, m, 0:w]).then_inc(rbc_act, 1)

            def copy_y(i):
                act.wait_ge(y_pe, i + 1)
                nc.scalar.copy(yT[:, bass.ds(i * PT, PT)], misc[:, 0, 0:PT]).then_inc(y_act, 1)

            def half(i, a, first=False, last=False):
                b = i * 2 + a
                for t in range(NT):
                    g = b * NT + t
                    u = (a + t) % 2
                    before = not (first and t == 0)
                    if before:
                        hi_probs(g - 1, 1 - u, (t - 1) % NT, 0)
                    exp_tile(g, u, a, t)
                    if before:
                        hi_probs(g - 1, 1 - u, (t - 1) % NT, 1)
                        hi_probs(g - 1, 1 - u, (t - 1) % NT, 2)
                    if first:
                        if t == 0:
                            copy_out(10, wvT[:, 0:4, :], ACC)
                            hi_qk(0, 2, 0)
                        if t == 1:
                            hi_qk(0, 3, 1)
                        if t == 2:
                            copy_out(12, wvo[:, 0:8:2, :], ACC)
                            hi_ctx(1, 1, 0, 1)
                        if t == 3:
                            copy_out(14, wvo[:, 1:8:2, :], ACC)
                            hi_ctx(1, 1, 1, 0)
                        if t == 4:
                            hi_ctx(1, 1, 2, 1)
                    if a == 1 and t == 0 and not last:
                        hi_qk(i + 1, 0, 0)
                    if t == 1 and not first:
                        copy_rbc(b * 2, 1, a)
                    if 2 <= t <= 4 and not last and not first:
                        hi_ctx(b + 1, 1 - a, t - 2, (t - 1 + a) % 2)
                    if a == 1 and 4 <= t <= 6 and not last:
                        hi_qk(i + 1, t - 3, (t - 3) % 2)
                    if t == 6:
                        if a == 0 and not first:
                            copy_y(i - 1)
                        copy_rbc(b * 2 + 1, 0, 1 - a)

            for k in range(2):
                hi_ctx(0, 0, k, (1 + k) % 2)
            copy_out(3, wqT[:, 4:8, :], S1)
            hi_ctx(0, 0, 2, 1)
            copy_out(5, wkT[:, 4:8, :], T0)
            copy_out(6, wqk[:, 0:8:2, :], T1, SCALE)
            copy_out(8, wqk[:, 8:16:2, :], S0, SCALE)
            hi_qk(0, 0, 0)
            hi_qk(0, 1, 1)
            half(0, 0, first=True)
            half(0, 1)
            with act.Fori(1, LAST) as i:
                half(i, 0)
                half(i, 1)
            half(LAST, 0)
            half(LAST, 1, last=True)
            G = B * NT
            hi_probs(G - 1, 1, NT - 1, 0)
            hi_probs(G - 1, 1, NT - 1, 1)
            for n in range(2):
                act.wait_ge(phi_pe, n + 1)
                nc.scalar.copy(phiT[:, 512 * n:512 * n + 512], bank((S1, S2)[n])).then_inc(phi_cp, 1)
            hi_probs(G - 1, 1, NT - 1, 2)
            copy_rbc(2 * B, 1, 1)
            for n in range(2, 4):
                act.wait_ge(phi_pe, n + 1)
                nc.scalar.copy(phiT[:, 512 * n:512 * n + 512], bank((S1, S2)[n - 2])).then_inc(phi_cp, 1)

            def copy_x2nT(n, q0, q1):
                act.wait_ge(x2nT_pe, n)
                nc.scalar.copy(x2nT[:, PT * q0:PT * q1], misc[:, 0, PT * q0:PT * q1]).then_inc(x2nT_act, 1)

            def copy_logits(q):
                for c in range(LC):
                    act.wait_ge(logit_pe, LC * q + c + 1)
                    nc.scalar.copy(logit[q][:, 512 * c:512 * c + 512], bank(RING[c])[0:PT, :]).then_inc(logit_act, 1)

            def copy_combT(q):
                for r in range(4):
                    act.wait_ge(combT_pe, 4 * q + r + 1)
                    nc.scalar.copy(combT[:, 4 * r:4 * r + 4, PT * q:PT * q + PT],
                                   blocks4(bank(RING[r]), PT)).then_inc(combT_act, 1)

            def dispatch_exp(q):
                act.wait_ge(dsub_pool, q + 1)
                nc.scalar.activation(disp[q][:, :], disp[q][:, :], ACT.Exp).then_inc(dexp_act, 1)

            def combine_exp(q):
                act.wait_ge(csub_dve, q + 1)
                nc.scalar.activation(comb[q][:, :], comb[q][:, :], ACT.Exp).then_inc(cexp_act, 1)

            copy_x2nT(1, 0, LAST)
            copy_logits(0)
            dispatch_exp(0)
            copy_logits(1)
            copy_y(LAST)
            combine_exp(0)
            copy_x2nT(2, LAST, NQ)
            copy_logits(2)
            dispatch_exp(1)
            combine_exp(1)
            copy_combT(0)
            dispatch_exp(2)
            copy_logits(3)
            combine_exp(2)
            copy_combT(1)
            dispatch_exp(3)
            combine_exp(3)
            copy_combT(2)
            copy_combT(3)
            for r in range(4):
                act.wait_ge(nb_dve, r + 1)
                for k in range(4 * r, 4 * r + 4):
                    nc.scalar.activation(xt[:, k, :], xt[:, k, :], ACT.Tanh, bias=xt_nb[:, k:k + 1],
                                         scale=xt_rs[:, k:k + 1]).then_inc(tanh_act, 1)
                if r >= 1:
                    act.wait_ge(xtT_pe, r)
                    nc.scalar.copy(xtT[:, 4 * r - 4:4 * r, :], blocks4(bank(RING[r - 1]))).then_inc(xtT_act, 1)
            act.wait_ge(xtT_pe, 4)
            nc.scalar.copy(xtT[:, 12:16, :], blocks4(bank(RING[3]))).then_inc(xtT_act, 1)
            act.wait_ge(y2_pe, 1)
            nc.scalar.copy(y2T[:, :], bank(S0)[:, 0:TOK]).then_inc(y2_act, 1)

        @block.vector
        def _(dve):
            v = nc.vector

            def layernorm(n, src, dst, q0, q1, done):
                for q in range(q0, q1):
                    s = v.bn_stats(lnbuf[:, q, :], src[:, q, :])
                s.then_inc(ln_stat, 1)
                dve.wait_ge(ln_stat, n + 1)
                for q in range(q0, q1):
                    s = v.bn_aggr(lnmv[:, q, :], lnbuf[:, q, :])
                s.then_inc(ln_mv, 1)
                dve.wait_ge(ln_mv, n + 1)
                v.tensor_scalar_add(lnvar[:, q0:q1], lnmv[:, q0:q1, 1], EPS).then_inc(ln_var, 1)
                if n == 0:
                    dve.wait_ge(ln_std, 1)
                    v.reciprocal(lnrs[:, :], lnvar[:, :]).then_inc(ln_rs, 1)

            def layernorm_apply(n, src, dst, q0, q1, done):
                dve.wait_ge(ln_rs, n + 1)
                for q in range(q0, q1):
                    s = v.tensor_scalar(dst[:, q, :], src[:, q, :], lnmv[:, q, 0:1], lnrs[:, q:q + 1],
                                        ALU.subtract, ALU.mult)
                s.then_inc(done, 1)

            dve.wait_ge(x_in, 16)
            layernorm(0, x_sb, xn, 0, NQ, xn_ready)
            layernorm_apply(0, x_sb, xn, 0, NQ, xn_ready)

            def copy_out(n, dst, k, scale=None):
                dve.wait_ge(setup_pe, n)
                if scale:
                    return v.tensor_scalar(dst, blocks4(bank(k)), scale, None, ALU.mult).then_inc(setup_dve, 1)
                return v.tensor_copy(dst, blocks4(bank(k))).then_inc(setup_dve, 1)

            def lo_ctx(b, a, k, m):
                dve.wait_ge(ctxT_hi, KB * b + (k + 1))
                cols = slice(KW * k, KW * k + KW)
                v.tensor_tensor(ctx_tl[a][:, cols], misc[:, m, 0:KW], ctx_th[a][:, cols].bitcast(F32),
                                ALU.subtract).then_inc(ctxT_lo, 1)

            def lo_qk(i, r, m):
                dve.wait_ge(qk_hi, i * 4 + (r + 1))
                both = misc[:, m, 0:4 * PT].rearrange("p (h b t) -> p b h t", h=4, b=2)
                hs = slice(4 * r, 4 * r + 4)
                v.tensor_tensor(qk_l[0][:, hs, :], both[:, 0], qk_h[0][:, hs, :].bitcast(F32),
                                ALU.subtract).then_inc(qk_lo, 1)

            def row_max(g, u):
                for k in range(KB):
                    dve.wait_ge(scores_pe, KB * g + (k + 1))
                    m = v.tensor_reduce(bankmax[:, u, k:k + 1], scores[:, k, 0:KW], AX.X, ALU.max)
                m.then_inc(bmax_dve, 1)
                dve.wait_ge(bmax_dve, g + 1)
                v.tensor_reduce(negmax[:, u:u + 1], bankmax[:, u, :], AX.X, ALU.max,
                                negate=True).then_inc(negmax_dve, 1)

            def lo_probs(g, u, t, k):
                dve.wait_ge(pT_hi, KB * g + (k + 1))
                dst = slice(CPB * k, CPB * k + CPB)
                v.tensor_tensor(pT_l[0:CK, t, dst, :],
                                turned[0:CK, (KB * u + k) % 2, :].rearrange("p (c r) -> p c r", c=CPB),
                                pT_h[0:CK, t, dst, :].bitcast(F32), ALU.subtract).then_inc(pT_lo, 1)

            def invert(g, a, grp):
                t0, t1 = GROUPS[grp]
                dve.wait_ge(exp_act, g)
                v.reciprocal(rden[:, a * NT + t0:a * NT + t1], den[:, a * NT + t0:a * NT + t1]
                             ).then_inc(rden_dve, 1)

            def normalise(n, a, grp):
                dve.wait_ge(rbc_act, n)
                dve.wait_ge(pv_pe, n)
                t0, t1 = GROUPS[grp]
                w = 128 * (t1 - t0)
                v.tensor_tensor(oT_cols[:, a, 128 * t0:128 * t1], acc[:, 0:w], rbc[:, 0:w],
                                ALU.mult).then_inc(oT_dve, 1)

            def half(i, a, first=False, last=False):
                b = i * 2 + a
                for t in range(NT):
                    g = b * NT + t
                    u = (a + t) % 2
                    if t == 1 and not first:
                        normalise(b * 2 - 1, 1 - a, 0)
                        invert(b * NT, 1 - a, 1)
                    if t == 4 and not first:
                        normalise(b * 2, 1 - a, 1)
                    row_max(g, u)
                    if not (first and t == 0):
                        for k in range(KB):
                            lo_probs(g - 1, 1 - u, (t - 1) % NT, k)
                    if first:
                        if t == 0:
                            lo_qk(0, 2, 0)
                        if t == 1:
                            copy_out(11, wvT[:, 4:8, :], ACC)
                            lo_qk(0, 3, 1)
                        if t == 2:
                            copy_out(13, wvo[:, 8:16:2, :], M0)
                            lo_ctx(1, 1, 0, 1)
                        if t == 3:
                            lo_ctx(1, 1, 1, 0)
                            copy_out(15, wvo[:, 9:16:2, :], M1)
                        if t == 4:
                            lo_ctx(1, 1, 2, 1)
                    if a == 1 and t == 0 and not last:
                        lo_qk(i + 1, 0, 0)
                    if 2 <= t <= 4 and not last and not first:
                        lo_ctx(b + 1, 1 - a, t - 2, (t - 1 + a) % 2)
                    if a == 1 and 4 <= t <= 6 and not last:
                        lo_qk(i + 1, t - 3, (t - 3) % 2)
                    if t == 5:
                        invert(b * NT + 3, a, 0)

            dve.wait_ge(setup_pe, 1)
            v.tensor_copy(xnT[:, :], bank(ACC)[:, 0:TOK]).then_inc(setup_dve, 1)
            lo_ctx(0, 0, 0, 1)
            lo_ctx(0, 0, 1, 0)
            copy_out(2, wqT[:, 0:4, :], S0)
            lo_ctx(0, 0, 2, 1)
            copy_out(4, wkT[:, 0:4, :], S2)
            copy_out(7, wqk[:, 1:8:2, :], ACC, SCALE)
            copy_out(9, wqk[:, 9:16:2, :], S1, SCALE)
            lo_qk(0, 0, 0)
            lo_qk(0, 1, 1)
            half(0, 0, first=True)
            half(0, 1)
            with dve.Fori(1, LAST) as i:
                half(i, 0)
                half(i, 1)
            half(LAST, 0)
            half(LAST, 1, last=True)

            def residual(n, q0, q1):
                dve.wait_ge(yturn_pe, n)
                v.tensor_tensor(x1[:, q0:q1, :], x_sb[:, q0:q1, :],
                                bank(S0)[0:PT, D * q0:D * q1].rearrange("p (q d) -> p q d", d=D),
                                ALU.add).then_inc(x1_dve, 1)
                dve.wait_ge(x1_dve, n)

            G = B * NT
            invert(G, 1, 1)
            normalise(2 * B - 1, 1, 0)
            lo_probs(G - 1, 1, NT - 1, 0)
            lo_probs(G - 1, 1, NT - 1, 1)
            residual(1, 0, LAST)
            layernorm(1, x1, x2n, 0, LAST, x2n_dve)
            lo_probs(G - 1, 1, NT - 1, 2)
            layernorm_apply(1, x1, x2n, 0, LAST, x2n_dve)

            def by_expert(ap):
                return ap[:, :].rearrange("p (n s) -> p n s", n=N_EXP)

            def by_slot(ap):
                return ap[:, :].rearrange("p (n s) -> p s n", n=N_EXP)

            def maxima(q):
                dve.wait_ge(logit_act, LC * (q + 1))
                v.tensor_reduce(dmax[q][:, :], by_expert(logit[q]), AX.X, ALU.max).then_inc(dmax_dve, 1)
                v.tensor_reduce(cmax[q][:, :], by_slot(logit[q]), AX.X, ALU.max).then_inc(cmax_dve, 1)

            def combine_shift(q):
                dve.wait_ge(cmax_dve, q + 1)
                dve.wait_ge(dsub_pool, q + 1)
                v.tensor_tensor(by_expert(comb[q]), by_expert(logit[q]),
                                cmax[q][:, :].unsqueeze(1).broadcast_to([PT, N_EXP, P_SLOT]),
                                ALU.subtract).then_inc(csub_dve, 1)

            def dispatch_sum(q):
                dve.wait_ge(dexp_act, q + 1)
                v.tensor_reduce(dsum[q][:, :], by_expert(disp[q]), AX.X, ALU.add).then_inc(dsum_dve, 1)
                dve.wait_ge(dsum_dve, q + 1)
                v.reciprocal(dsum[q][:, :], dsum[q][:, :]).then_inc(drec_dve, 1)

            def combine_sum(q):
                dve.wait_ge(cexp_act, q + 1)
                v.tensor_reduce(csum[q][:, :], by_slot(comb[q]), AX.X, ALU.add).then_inc(csum_dve, 1)
                dve.wait_ge(csum_dve, q + 1)
                v.reciprocal(csum[q][:, :], csum[q][:, :]).then_inc(crec_dve, 1)

            maxima(0)
            combine_shift(0)
            dispatch_sum(0)
            normalise(2 * B, 1, 1)
            maxima(1)
            residual(2, LAST, NQ)
            layernorm(2, x1, x2n, LAST, NQ, x2n_dve)
            combine_shift(1)
            layernorm_apply(2, x1, x2n, LAST, NQ, x2n_dve)
            combine_sum(0)
            dispatch_sum(1)
            maxima(2)
            combine_shift(2)
            combine_sum(1)
            dispatch_sum(2)
            maxima(3)
            combine_shift(3)
            dispatch_sum(3)
            combine_sum(2)
            combine_sum(3)

            def slot_stats(r):
                ks = slice(4 * r, 4 * r + 4)
                dve.wait_ge(xt_pe, r + 1)
                v.tensor_scalar(xt[:, ks, :], blocks4(bank(SLOT_BANKS[r])), -33000.0, 65000.0,
                                ALU.max, ALU.min).then_inc(clip_dve, 1)
                dve.wait_ge(clip_dve, r + 1)
                for k in range(4 * r, 4 * r + 4):
                    s = v.bn_stats(xt_st[:, k, :], xt[:, k, :])
                s.then_inc(stat_dve, 1)
                dve.wait_ge(stat_dve, r + 1)
                for k in range(4 * r, 4 * r + 4):
                    s = v.bn_aggr(xt_mv[:, k, :], xt_st[:, k, :])
                s.then_inc(mv_dve, 1)
                dve.wait_ge(mv_dve, r + 1)
                v.tensor_scalar_add(xt_var[:, ks], xt_mv[:, ks, 1], EPS).then_inc(var_dve, 1)

            def slot_bias(r):
                ks = slice(4 * r, 4 * r + 4)
                dve.wait_ge(rs_pool, r + 1)
                v.scalar_tensor_tensor(xt_nb[:, ks], xt_mv[:, ks, 0], -1.0, xt_rs[:, ks],
                                       ALU.mult, ALU.mult).then_inc(nb_dve, 1)

            def add_expert_bias(r):
                dve.wait_ge(yt_pe, r + 1)
                v.tensor_tensor(yt[:, 4 * r:4 * r + 4, :], blocks4(bank(SLOT_BANKS[r])),
                                eb[:, 4 * r:4 * r + 4, :], ALU.add).then_inc(yt_dve, 1)

            slot_stats(0)
            for r in range(1, 4):
                slot_stats(r)
                slot_bias(r - 1)
            slot_bias(3)
            dve.wait_ge(eb_in, 16 * EPT)
            for r in range(4):
                add_expert_bias(r)
            dve.wait_ge(y2turn_pe, 1)
            v.tensor_tensor(out_sb[:, :, :], x1[:, :, :], bank(T0)[0:PT, :].rearrange("p (q d) -> p q d", q=NQ),
                            ALU.add).then_inc(out_dve, 1)


_INS = ['x', 'ctx_1024', 'L0_xattn_Wq', 'L0_xattn_Wk', 'L0_xattn_Wv', 'L0_xattn_Wo',
        'L0_ffn_phi_w', 'L0_ffn_phi_b', 'L0_ffn_expert_w', 'L0_ffn_expert_b']
_OUTS = [((8, 56, 128), 'float32')]


def kernel(**inputs):
    import numpy as _np
    import concourse.bacc as _bacc
    from concourse import mybir as _mybir
    from concourse.bass_utils import run_bass_kernel_spmd as _run

    nc = _bacc.Bacc("TRN2", target_bir_lowering=False, num_devices=1)
    arrays, args = {}, []
    for name in _INS:
        a = _np.ascontiguousarray(inputs[name])
        arrays[f"in_{name}_dram"] = a
        args.append(nc.dram_tensor(f"in_{name}_dram", a.shape, _mybir.dt.from_np(a.dtype), kind="ExternalInput").ap())
    for i, (shape, dtype) in enumerate(_OUTS):
        dt = _mybir.dt.from_np(_np.dtype(dtype))
        args.append(nc.dram_tensor(f"out_{i}_dram", shape, dt, kind="ExternalOutput").ap())
    xattn_softmoe_kernel(nc, *args)
    r = _run(nc, [arrays], core_ids=[0])
    got = tuple(r.results[0][f"out_{i}_dram"] for i in range(len(_OUTS)))
    return got[0]
```

```python
from contextlib import ExitStack

import concourse.bass as bass
from concourse import mybir

F32 = mybir.dt.float32
F32R = mybir.dt.float32r
ALU = mybir.AluOpType
ACT = mybir.ActivationFunctionType
AX = mybir.AxisListType


def xattn_softmoe_kernel(
    nc: bass.Bass,
    x: bass.AP,
    ctx_1024: bass.AP,
    Wq: bass.AP,
    Wk: bass.AP,
    Wv: bass.AP,
    Wo: bass.AP,
    phi_w: bass.AP,
    phi_b: bass.AP,
    expert_w: bass.AP,
    expert_b: bass.AP,
    out: bass.AP,
):
    B, T, D = x.shape
    M = ctx_1024.shape[1]
    INNER = Wq.shape[1]
    DH = 64
    HEADS = INNER // DH
    ROWS = HEADS * T
    NT = ROWS // 128
    NC = 12
    CK = M // NC
    KB = 3
    KW = M // KB
    CPB = NC // KB
    PAIRS = B // 2
    PT = 2 * T
    TOK = B * T
    EPS = 1e-5
    SCALE = DH ** -0.5
    N_EXP, _, H = expert_w.shape
    SLOTS = phi_w.shape[0]
    P_SLOT = SLOTS // N_EXP
    NS = SLOTS // 128
    EPT = 128 // P_SLOT
    NQ = TOK // PT
    LC = SLOTS // 512
    BW = 256
    BR = SLOTS // BW
    assert ROWS == NT * 128 and NT == 7 and M == NC * CK and KW <= 512 and D == 128
    GROUPS = ((0, 3), (3, 7))

    def wait(eng, sem, value):
        if isinstance(value, int) and value <= 0:
            return
        eng.wait_ge(sem, value)

    with ExitStack() as ctx:
        def sem(name):
            return ctx.enter_context(nc.semaphore(name))

        def sb(name, shape, dt=F32):
            return ctx.enter_context(nc.sbuf_tensor(name, shape, dt))

        scores = ctx.enter_context(nc.psum_tensor("scores", [128, KB, 512], F32))
        turned = ctx.enter_context(nc.psum_tensor("turned", [128, 2, 512], F32))
        acc = ctx.enter_context(nc.psum_tensor("acc", [128, 512], F32))
        misc = ctx.enter_context(nc.psum_tensor("misc", [128, 2, 512], F32))

        ident = sb("ident", [128, 128])
        zero = sb("zero", [128, 1])
        neghalf = sb("neghalf", [128, NQ])
        x_sb = sb("x_sb", [PT, NQ, D])
        b_hl = sb("b_hl", [128, BW], F32R)
        pick = sb("pick", [128, BR], F32R)
        yT = sb("yT", [D, TOK])
        xnT = sb("xnT", [D, TOK])
        x2nT = xnT
        phiT = sb("phiT", [D, SLOTS])
        lnbuf = sb("lnbuf", [PT, NQ, 6])
        lnmv = sb("lnmv", [PT, NQ, 2])
        lnvar = sb("lnvar", [PT, NQ])
        lnrs = sb("lnrs", [PT, NQ])

        place = [(nc.sbuf_base + 63) // 64 * 64]

        def at(name, shape, dt, address):
            return nc.alloc_sbuf_tensor_at(name, shape, dt, offset=address)

        def nbytes(shape):
            n = 4
            for d in shape[1:]:
                n *= d
            return n

        def take(name, shape, dt=F32):
            address = place[0]
            place[0] += (nbytes(shape) + 31) // 32 * 32
            return at(name, shape, dt, address), address

        pT_h, pT_h_at = take("pT_h", [128, NT, NC, 128], F32R)
        pT_l, pT_l_at = take("pT_l", [128, NT, NC, 128], F32R)
        TILE = nbytes([1, NC, 128])
        prob0, prob_at = take("prob0", [128, M])
        prob = [prob0, take("prob1", [128, M])[0]]
        ctx_nh0, n0_at = take("ctx_nh0", [CK, NC, D], F32R)
        ctx_nl0, _ = take("ctx_nl0", [CK, NC, D], F32R)
        ctx_nh1, n1_at = take("ctx_nh1", [CK, NC, D], F32R)
        ctx_nl1, _ = take("ctx_nl1", [CK, NC, D], F32R)
        ctx_th1, _ = take("ctx_th1", [D, M], F32R)
        ctx_tl1, _ = take("ctx_tl1", [D, M], F32R)
        qk_h1, _ = take("qk_h1", [D, HEADS, T], F32R)
        qk_l1, _ = take("qk_l1", [D, HEADS, T], F32R)
        ctx_th0, t0_at = take("ctx_th0", [D, M], F32R)
        ctx_tl0, _ = take("ctx_tl0", [D, M], F32R)
        qk_h0, _ = take("qk_h0", [D, HEADS, T], F32R)
        qk_l0, _ = take("qk_l0", [D, HEADS, T], F32R)
        ctx_raw, _ = take("ctx_raw", [CK, NC, D])
        qk_raw, qk_raw_at = take("qk_raw", [D, HEADS, T])
        ctx_nh, ctx_nl, ctx_th, ctx_tl = [ctx_nh0, ctx_nh1], [ctx_nl0, ctx_nl1], [ctx_th0, ctx_th1], [ctx_tl0, ctx_tl1]
        qk_h, qk_l = [qk_h0, qk_h1], [qk_l0, qk_l1]
        wqk, wqk_at = take("wqk", [D, HEADS, D])
        wvo, _ = take("wvo", [D, HEADS, D])
        oT, oT_at = take("oT", [D, 2, HEADS, T])
        oT_cols = oT[:, :, :, :].rearrange("p b h t -> p b (h t)")
        rbc, rbc_at = take("rbc", [128, 512])
        bankmax, _ = take("bankmax", [128, 2, KB])
        negmax, _ = take("negmax", [128, 2])
        den, _ = take("den", [128, 2 * NT])
        rden, _ = take("rden", [128, 2 * NT])
        assert place[0] <= nc.sbuf_usable_end

        KB4 = 4096
        wq_sb = at("wq_sb", [D, INNER], F32, pT_h_at)
        wk_sb = at("wk_sb", [D, INNER], F32, pT_h_at + KB4)
        wqT = at("wqT", [128, HEADS // 2, D], F32, pT_h_at + 2 * KB4)
        wkT = at("wkT", [128, HEADS // 2, D], F32, pT_h_at + 3 * KB4)
        xn = at("xn", [PT, NQ, D], F32, pT_h_at + 4 * KB4)
        wv_sb = at("wv_sb", [D, INNER], F32, pT_h_at + 3 * TILE)
        wo_sb = at("wo_sb", [128, HEADS // 2, D], F32, pT_h_at + 3 * TILE + KB4)
        wvT = at("wvT", [128, HEADS // 2, D], F32, pT_h_at + 3 * TILE + 2 * KB4)

        KB8 = 8192
        phi_sb = at("phi_sb", [128, NS, D], F32, wqk_at)
        x2n = at("x2n", [PT, NQ, D], F32, qk_raw_at)
        b_raw = at("b_raw", [128, BW], F32, qk_raw_at + 2048)
        logit = [at("logit0", [PT, SLOTS], F32, wqk_at), at("logit1", [PT, SLOTS], F32, t0_at + KB8),
                 at("logit2", [PT, SLOTS], F32, n0_at), at("logit3", [PT, SLOTS], F32, pT_h_at + KB8)]
        disp = [at("disp0", [PT, SLOTS], F32, t0_at), at("disp1", [PT, SLOTS], F32, t0_at + 2 * KB8),
                at("disp2", [PT, SLOTS], F32, pT_h_at), at("disp3", [PT, SLOTS], F32, pT_l_at + 2048)]
        comb = logit
        stats_at = [qk_raw_at + 2048, qk_raw_at + 2816, n0_at + KB8, n0_at + KB8 + 768]
        dmax = [at(f"dmax{q}", [PT, N_EXP], F32, stats_at[q]) for q in range(NQ)]
        dsum = [at(f"dsum{q}", [PT, N_EXP], F32, stats_at[q] + 256) for q in range(NQ)]
        cmax = [at(f"cmax{q}", [PT, P_SLOT], F32, stats_at[q] + 512) for q in range(NQ)]
        csum = [at(f"csum{q}", [PT, P_SLOT], F32, stats_at[q] + 640) for q in range(NQ)]
        combT = at("combT", [128, NS, TOK], F32, pT_h_at + 2 * KB8)
        ew = at("ew", [D, N_EXP, H], F32, pT_l_at + 3 * TILE)
        eb = at("eb", [128, NS, H], F32, n1_at)
        xt = at("xt", [128, NS, D], F32, t0_at)
        xtT = at("xtT", [128, NS, 128], F32, wqk_at)
        yt = at("yt", [128, NS, H], F32, t0_at + 2 * KB8)
        y2T = at("y2T", [H, TOK], F32, oT_at)
        out_sb = at("out_sb", [PT, NQ, D], F32, oT_at + 2048)
        xt_st = at("xt_st", [128, NS, 6], F32, rbc_at)
        xt_mv = at("xt_mv", [128, NS, 2], F32, rbc_at + 384)
        xt_var = at("xt_var", [128, NS], F32, rbc_at + 512)
        xt_rs = at("xt_rs", [128, NS], F32, rbc_at + 576)
        xt_nb = at("xt_nb", [128, NS], F32, rbc_at + 640)

        x_in = sem("x_in")
        wq_in = sem("wq_in")
        wk_in = sem("wk_in")
        wvo_in = sem("wvo_in")
        zeroed = sem("zeroed")
        ident_ready = sem("ident_ready")
        ln_stat = sem("ln_stat")
        ln_mv = sem("ln_mv")
        ln_var = sem("ln_var")
        ln_std = sem("ln_std")
        ln_rs = sem("ln_rs")
        xn_ready = sem("xn_ready")
        setup_pe = sem("setup_pe")
        setup_act = sem("setup_act")
        setup_dve = sem("setup_dve")
        ctx0_in = [sem(f"ctx0_in{k}") for k in range(KB)]
        ctx_in = sem("ctx_in")
        ctx_nat = sem("ctx_nat")
        nat_hi = sem("nat_hi")
        ctxT_pe = sem("ctxT_pe")
        ctxT_hi = sem("ctxT_hi")
        ctxT_lo = sem("ctxT_lo")
        qk_pe = sem("qk_pe")
        qk_hi = sem("qk_hi")
        qk_lo = sem("qk_lo")
        qkb_hi = sem("qkb_hi")
        qkb_lo = sem("qkb_lo")
        scores_pe = sem("scores_pe")
        bmax_dve = sem("bmax_dve")
        negmax_dve = sem("negmax_dve")
        exp_act = sem("exp_act")
        turned_pe = sem("turned_pe")
        pT_hi = sem("pT_hi")
        pT_lo = sem("pT_lo")
        pv_pe = sem("pv_pe")
        rden_dve = sem("rden_dve")
        rbc_pe = sem("rbc_pe")
        rbc_act = sem("rbc_act")
        oT_dve = sem("oT_dve")
        y_pe = sem("y_pe")
        y_act = sem("y_act")
        bias_in = sem("bias_in")
        phi_in = sem("phi_in")
        ew_in = sem("ew_in")
        eb_in = sem("eb_in")
        bias_zero = sem("bias_zero")
        pick_ready = sem("pick_ready")
        bias_hi = sem("bias_hi")
        bias_lo = sem("bias_lo")
        phi_pe = sem("phi_pe")
        phi_cp = sem("phi_cp")
        yturn_pe = sem("yturn_pe")
        x1_dve = sem("x1_dve")
        x2n_dve = sem("x2n_dve")
        x2nT_pe = sem("x2nT_pe")
        x2nT_act = sem("x2nT_act")
        logit_pe = sem("logit_pe")
        logit_act = sem("logit_act")
        dmax_dve = sem("dmax_dve")
        cmax_dve = sem("cmax_dve")
        dsub_pool = sem("dsub_pool")
        csub_dve = sem("csub_dve")
        csub_pool = sem("csub_pool")
        dexp_act = sem("dexp_act")
        cexp_act = sem("cexp_act")
        dsum_dve = sem("dsum_dve")
        csum_dve = sem("csum_dve")
        drec_dve = sem("drec_dve")
        crec_dve = sem("crec_dve")
        disp_pool = sem("disp_pool")
        comb_pool = sem("comb_pool")
        comb_dve = sem("comb_dve")
        last_dmax = sem("last_dmax")
        last_dsub = sem("last_dsub")
        last_dexp = sem("last_dexp")
        last_dsum = sem("last_dsum")
        last_drec = sem("last_drec")
        last_disp = sem("last_disp")
        combT_pe = sem("combT_pe")
        combT_act = sem("combT_act")
        xt_pe = sem("xt_pe")
        clip_dve = sem("clip_dve")
        stat_dve = sem("stat_dve")
        mv_dve = sem("mv_dve")
        var_dve = sem("var_dve")
        rs_pool = sem("rs_pool")
        nb_dve = sem("nb_dve")
        tanh_act = sem("tanh_act")
        xtT_pe = sem("xtT_pe")
        xtT_act = sem("xtT_act")
        yt_pe = sem("yt_pe")
        yt_dve = sem("yt_dve")
        y2_pe = sem("y2_pe")
        y2_act = sem("y2_act")
        y2turn_pe = sem("y2turn_pe")
        out_dve = sem("out_dve")
        stored = sem("stored")

        ctx_v = ctx_1024.rearrange("b (p j) d -> b p j d", j=NC)
        x_v = x.rearrange("(q b) t d -> (b t) q d", b=2)
        out_v = out.rearrange("(q b) t d -> (b t) q d", b=2)

        S0, S1, S2, T0, T1, ACC, M0, M1 = range(8)

        def bank(k):
            return [scores[:, 0, :], scores[:, 1, :], scores[:, 2, :], turned[:, 0, :],
                    turned[:, 1, :], acc[:, :], misc[:, 0, :], misc[:, 1, :]][k]

        RING = (T0, T1, S1, S2)
        LOGIT_BANKS = ((M0, M1, M0, M1), (M1, M0, M1, M0), (M0, M1, M1, S1), RING)
        SLOT_BANKS = (S0, ACC, M1, M0)

        def blocks4(ap, w=128):
            return ap[:, 0:4 * w].rearrange("p (h c) -> p h c", h=4)

        def rounds_of_qk(t):
            return min(4, -(-(-(-128 * (t + 1) // T)) // 4))

        LAST = PAIRS - 1
        HALF = SLOTS // 2
        OUT_BANKS = (M0, S0, ACC)
        PARTS = ((0, LAST - 1), (LAST - 1, LAST), (LAST, NQ))
        block = ctx.enter_context(nc.Block())

        @block.sync
        def _(sp):
            sp.dma_start(x_sb[:, :, :], x_v).then_inc(x_in, 16)
            for k in range(KB):
                chunks = slice(CPB * k, CPB * k + CPB)
                sp.dma_start(ctx_raw[:, chunks, :], ctx_v[0][:, chunks, :]).then_inc(ctx0_in[k], 16)

            def load_ctx(b):
                sp.wait_ge(ctxT_pe, KB * b)
                sp.wait_ge(ctx_nat, b)
                sp.dma_start(ctx_raw[:, :, :], ctx_v[b]).then_inc(ctx_in, 16)

            load_ctx(1)
            with sp.Fori(1, PAIRS) as i:
                load_ctx(2 * i)
                load_ctx(2 * i + 1)

            sp.wait_ge(qk_pe, 4 * PAIRS)
            sp.dma_start(phi_sb[:, :, :], phi_w.rearrange("(k p) d -> p k d", p=128)).then_inc(phi_in, 16)
            sp.wait_ge(bias_zero, 1)
            for p in (0, 32):
                sp.dma_start(b_raw[p:p + BR, :], phi_b.rearrange("(c e) -> c e", c=BR)).then_inc(bias_in, 16)
            sp.wait_ge(pv_pe, 2 * B)
            sp.dma_start(ew[:, :, :], expert_w.rearrange("n d h -> d n h")).then_inc(ew_in, 16)
            eb_v = expert_b.rearrange("(k n) h -> n k h", n=EPT)
            for n in range(EPT):
                sp.dma_start(eb[n * P_SLOT:(n + 1) * P_SLOT, :, :],
                             eb_v[n].partition_broadcast(P_SLOT)).then_inc(eb_in, 16)
            for part, (q0, q1) in enumerate(PARTS):
                sp.wait_ge(out_dve, part + 1)
                sp.dma_start(out_v[:, q0:q1, :], out_sb[:, q0:q1, :]).then_inc(stored, 16)
            sp.wait_ge(stored, 16 * len(PARTS))

        @block.gpsimd
        def _(pool):
            gp = nc.gpsimd
            gp.memset(ident[:, :], 0.0).then_inc(zeroed, 1)
            gp.memset(zero[:, :], 0.0).then_inc(zeroed, 1)
            gp.memset(neghalf[:, :], -0.5).then_inc(zeroed, 1)
            pool.wait_ge(zeroed, 3)
            gp.affine_select(out=ident[:, :], in_=ident[:, :], compare_op=ALU.not_equal,
                             fill=1.0, base=0, pattern=[[-1, 128]],
                             channel_multiplier=1).then_inc(ident_ready, 1)
            pool.wait_ge(ident_ready, 1)
            gp.tensor_tensor(pick[:, :], ident[:, 0:BR], ident[:, 32:32 + BR], ALU.add).then_inc(pick_ready, 1)

            def split_ctx(b, a, first=False):
                if first:
                    for k in range(KB):
                        pool.wait_ge(ctx0_in[k], 16)
                else:
                    pool.wait_ge(ctx_in, 16 * b)
                wait(pool, pv_pe, 2 * (b - 1))
                gp.tensor_tensor(ctx_nh[a][:, :, :].rearrange("p j d -> p (j d)"),
                                 ctx_raw[:, :, :].rearrange("p j d -> p (j d)"),
                                 zero[0:CK, :].broadcast_to([CK, NC * D]), ALU.add).then_inc(nat_hi, 1)
                pool.wait_ge(nat_hi, b + 1)
                gp.tensor_tensor(ctx_nl[a][:, :, :], ctx_raw[:, :, :],
                                 ctx_nh[a][:, :, :].bitcast(F32), ALU.subtract).then_inc(ctx_nat, 1)

            def split_qk(i):
                pool.wait_ge(qk_lo, 4 * (i + 1))
                wait(pool, scores_pe, KB * 2 * NT * i)
                gp.tensor_tensor(qk_h[1][:, :, :].rearrange("p h t -> p (h t)"),
                                 qk_raw[:, :, :].rearrange("p h t -> p (h t)"),
                                 zero[:, :].broadcast_to([D, ROWS]), ALU.add).then_inc(qkb_hi, 1)
                pool.wait_ge(qkb_hi, i + 1)
                gp.tensor_tensor(qk_l[1][:, :, :], qk_raw[:, :, :],
                                 qk_h[1][:, :, :].bitcast(F32), ALU.subtract).then_inc(qkb_lo, 1)

            def pair(i):
                split_qk(i)
                split_ctx(2 * i + 1, 1)
                split_ctx(2 * i + 2, 0)

            def root(n, q0, q1):
                pool.wait_ge(ln_var, n + 1)
                gp.tensor_tensor(lnrs[:, q0:q1], lnvar[:, q0:q1], neghalf[0:PT, q0:q1],
                                 ALU.pow).then_inc(ln_rs, 1)

            def by_expert(ap):
                return ap[:, :].rearrange("p (n s) -> p n s", n=N_EXP)

            def dispatch_shift(q):
                pool.wait_ge(dmax_dve, q + 1)
                gp.tensor_tensor(by_expert(disp[q]), by_expert(logit[q]),
                                 dmax[q][:, :].unsqueeze(2).broadcast_to([PT, N_EXP, P_SLOT]),
                                 ALU.subtract).then_inc(dsub_pool, 1)

            def dispatch_scale(q):
                pool.wait_ge(drec_dve, q + 1)
                gp.tensor_tensor(by_expert(disp[q]), by_expert(disp[q]),
                                 dsum[q][:, :].unsqueeze(2).broadcast_to([PT, N_EXP, P_SLOT]),
                                 ALU.mult).then_inc(disp_pool, 1)

            def combine_scale(q, end=SLOTS):
                pool.wait_ge(crec_dve, q + 1)
                part = comb[q][:, 0:end].rearrange("p (n s) -> p n s", s=P_SLOT)
                gp.tensor_tensor(part, part,
                                 csum[q][:, :].unsqueeze(1).broadcast_to([PT, end // P_SLOT, P_SLOT]),
                                 ALU.mult).then_inc(comb_pool, 1)

            def combine_shift(q):
                pool.wait_ge(cmax_dve, q + 1)
                if q == LAST:
                    pool.wait_ge(last_dsub, LC)
                gp.tensor_tensor(by_expert(comb[q]), by_expert(logit[q]),
                                 cmax[q][:, :].unsqueeze(1).broadcast_to([PT, N_EXP, P_SLOT]),
                                 ALU.subtract).then_inc(csub_pool, 1)

            def slot_root(r):
                pool.wait_ge(var_dve, r + 1)
                gp.tensor_tensor(xt_rs[:, 4 * r:4 * r + 4], xt_var[:, 4 * r:4 * r + 4], neghalf[:, 0:4],
                                 ALU.pow).then_inc(rs_pool, 1)

            split_ctx(0, 0, first=True)
            pair(0)
            with pool.Fori(1, LAST) as i:
                pair(i)
            split_qk(LAST)
            pool.wait_ge(qkb_lo, PAIRS)
            gp.memset(b_raw[:, :], 0.0).then_inc(bias_zero, 1)
            root(1, 0, 2)
            split_ctx(B - 1, 1)
            pool.wait_ge(bias_in, 32)
            gp.tensor_tensor(b_hl[:, :], b_raw[:, :], zero[:, :].broadcast_to([128, BW]),
                             ALU.add).then_inc(bias_hi, 1)
            pool.wait_ge(bias_hi, 1)
            gp.tensor_tensor(b_hl[32:64, :], b_raw[32:64, :], b_hl[32:64, :].bitcast(F32),
                             ALU.subtract).then_inc(bias_lo, 1)

            dispatch_shift(0)
            root(2, 2, LAST)
            dispatch_scale(0)
            combine_scale(0)
            dispatch_shift(1)
            dispatch_scale(1)
            dispatch_shift(2)
            root(3, LAST, NQ)
            combine_scale(1)
            dispatch_scale(2)
            combine_shift(2)
            slot_root(0)
            combine_shift(LAST)
            slot_root(1)
            slot_root(2)
            slot_root(3)
            combine_scale(2, HALF)
            combine_scale(LAST, HALF)

        @block.tensor
        def _(pe):
            mm = nc.tensor.matmul
            tr = nc.tensor.transpose

            def turn_ctx(b, k, m, first=False):
                if first:
                    pe.wait_ge(ctx0_in[k], 16)
                else:
                    pe.wait_ge(ctx_in, 16 * b)
                for c in range(CPB):
                    last = tr(misc[:, m, CK * c:CK * c + CK], ctx_raw[:, CPB * k + c, :], ident[0:CK, 0:CK])
                last.then_inc(ctxT_pe, 1)

            def make_qk(i, r, m):
                for c in range(4):
                    last = mm(misc[:, m, PT * c:PT * c + PT], wqk[:, 4 * r + c, :],
                              xnT[:, bass.ds(i * PT, PT)], start=True, stop=True)
                last.then_inc(qk_pe, 1)

            def turn_weight(w, half, k):
                for c in range(4):
                    j = 4 * half + c
                    last = tr(bank(k)[:, 128 * c:128 * c + 128], w[:, 128 * j:128 * j + 128], ident[:, :])
                last.then_inc(setup_pe, 1)

            def head_products(wT, right, r, k):
                p = DH * (r % 2)
                for c in range(4):
                    j = r // 2 * 4 + c
                    last = mm(bank(k)[:, 128 * c:128 * c + 128], wT[p:p + DH, j, :],
                              right[p:p + DH, j, :], start=True, stop=True)
                last.then_inc(setup_pe, 1)

            pe.wait_ge(ident_ready, 1)
            pe.wait_ge(wq_in, 16)
            turn_weight(wq_sb, 0, S0)
            turn_weight(wq_sb, 1, S1)
            turn_ctx(0, 0, 1, first=True)
            pe.wait_ge(xn_ready, 1)
            for q in range(NQ):
                last = tr(bank(ACC)[:, PT * q:PT * q + PT], xn[:, q, :], ident[0:PT, 0:PT])
            last.then_inc(setup_pe, 1)
            turn_ctx(0, 1, 0, first=True)
            pe.wait_ge(wk_in, 16)
            turn_weight(wk_sb, 0, S2)
            turn_weight(wk_sb, 1, T0)
            pe.wait_ge(ctxT_lo, 1)
            turn_ctx(0, 2, 1, first=True)
            pe.wait_ge(setup_dve, 3)
            head_products(wqT, wkT, 0, T1)
            head_products(wqT, wkT, 1, ACC)
            pe.wait_ge(setup_act, 2)
            head_products(wqT, wkT, 2, T0)
            pe.wait_ge(setup_act, 3)
            pe.wait_ge(setup_dve, 4)
            pe.wait_ge(ctxT_lo, 2)
            make_qk(0, 0, 0)
            pe.wait_ge(ctxT_lo, 3)
            make_qk(0, 1, 1)

            def make_scores(g, a, t):
                wait(pe, exp_act, g)
                rows = slice(128 * t, 128 * t + 128)
                hi = qk_h[a][:, :, :].rearrange("p h t -> p (h t)")[:, rows]
                lo = qk_l[a][:, :, :].rearrange("p h t -> p (h t)")[:, rows]
                for k in range(KB):
                    o = scores[:, k, 0:KW]
                    keys = slice(KW * k, KW * k + KW)
                    mm(o, hi, ctx_th[a][:, keys], start=True, stop=False)
                    mm(o, hi, ctx_tl[a][:, keys], start=False, stop=False)
                    mm(o, lo, ctx_th[a][:, keys], start=False, stop=True).then_inc(scores_pe, 1)

            def turn_probs(g, u, k):
                m = (KB * u + k) % 2
                wait(pe, pT_lo, KB * g + k - 1)
                if k == 0:
                    pe.wait_ge(exp_act, g + 1)
                for c in range(CPB):
                    j = CPB * k + c
                    last = tr(turned[0:CK, m, 128 * c:128 * c + 128], prob[u][:, CK * j:CK * j + CK],
                              ident[:, :])
                last.then_inc(turned_pe, 1)

            def context_product(b, a, grp, chunks, by_bank=False):
                t0, t1 = GROUPS[grp]
                o = acc[:, 0:128 * (t1 - t0)].rearrange("p (t r) -> p t r", r=128)
                if chunks[0] == 0:
                    if not by_bank:
                        pe.wait_ge(pT_lo, KB * (b * NT + t1))
                    pe.wait_ge(ctx_nat, b + 1)
                    wait(pe, oT_dve, b * 2 + grp)
                for j in chunks:
                    if by_bank and j % CPB == 0:
                        pe.wait_ge(pT_lo, KB * (b * NT + t1 - 1) + j // CPB + 1)
                    hi, lo = pT_h[0:CK, t0:t1, j, :], pT_l[0:CK, t0:t1, j, :]
                    mm(o, ctx_nh[a][:, j, :], hi, start=(j == 0), stop=False)
                    mm(o, ctx_nh[a][:, j, :], lo, start=False, stop=False)
                    last = mm(o, ctx_nl[a][:, j, :], hi, start=False, stop=(j == NC - 1))
                if chunks[-1] == NC - 1:
                    last.then_inc(pv_pe, 1)

            def spread_rden(a, grp, m):
                t0, t1 = GROUPS[grp]
                for t in range(t0, t1):
                    last = tr(misc[:, m, 128 * (t - t0):128 * (t - t0) + 128],
                              rden[:, a * NT + t:a * NT + t + 1].broadcast_to([128, 128]), ident[:, :])
                last.then_inc(rbc_pe, 1)

            def project(r):
                for h in range(8 * r, 8 * r + 8):
                    last = mm(misc[:, 0, 0:PT].rearrange("p (b t) -> p b t", b=2), wvo[:, h, :],
                              oT[:, :, h, :], start=(h == 0), stop=(h == HEADS - 1))
                return last

            def turn_phi(n, k):
                for c in range(4):
                    last = tr(bank(k)[:, 128 * c:128 * c + 128], phi_sb[:, 4 * n + c, :], ident[:, :])
                last.then_inc(phi_pe, 1)

            def turn_y(q0, q1, k):
                for q in range(q0, q1):
                    last = tr(bank(k)[0:PT, D * (q - q0):D * (q - q0) + D], yT[:, PT * q:PT * q + PT], ident[:, :])
                last.then_inc(yturn_pe, 1)

            def turn_x2n(n, q0, q1, k):
                pe.wait_ge(x2n_dve, n)
                for q in range(q0, q1):
                    last = tr(bank(k)[:, PT * (q - q0):PT * (q - q0) + PT], x2n[:, q, :], ident[0:PT, 0:PT])
                last.then_inc(x2nT_pe, 1)

            def logits(q, c):
                o = bank(LOGIT_BANKS[q][c])[0:PT, :]
                mm(o, x2nT[:, PT * q:PT * q + PT], phiT[:, 512 * c:512 * c + 512], start=True, stop=False)
                for e in range(512 // BW):
                    row = 512 // BW * c + e
                    last = mm(o[:, BW * e:BW * e + BW], pick[:, row:row + 1].broadcast_to([128, PT]),
                              b_hl[:, :], start=False, stop=(e == 512 // BW - 1))
                last.then_inc(logit_pe, 1)

            def early(a, t, mid):
                b = B - 2 + a
                step = (a, t, mid)
                if step == (0, 0, True):
                    pe.wait_ge(rbc_act, 2 * b - 1)
                    pe.wait_ge(y_act, 2)
                    turn_y(0, 2, M0)
                if step == (0, 0, False):
                    pe.wait_ge(qk_lo, 4 * PAIRS)
                    pe.wait_ge(phi_in, 16)
                    turn_phi(0, M1)
                if step == (0, 1, True):
                    pe.wait_ge(phi_cp, 1)
                    turn_phi(1, M1)
                if step == (0, 2, True):
                    pe.wait_ge(rbc_act, 2 * b)
                    turn_phi(2, M0)
                if step == (0, 3, True):
                    pe.wait_ge(phi_cp, 3)
                    turn_phi(3, M0)
                if step == (0, 4, True):
                    pe.wait_ge(ctxT_lo, KB * (b + 1) + 1)
                    turn_x2n(1, 0, 2, M1)
                if step == (0, 5, True):
                    pe.wait_ge(ctxT_lo, KB * (b + 1) + 2)
                    pe.wait_ge(phi_cp, 4)
                    pe.wait_ge(x2nT_act, 1)
                    pe.wait_ge(bias_lo, 1)
                    pe.wait_ge(pick_ready, 1)
                    logits(0, 0)
                if step == (0, 6, True):
                    pe.wait_ge(ctxT_lo, KB * (b + 1) + 3)
                    logits(0, 1)
                if step == (1, 0, True):
                    pe.wait_ge(y_act, LAST)
                    logits(0, 2)
                if step == (1, 0, False):
                    pe.wait_ge(rbc_act, 2 * b - 1)
                    logits(0, 3)
                if step == (1, 1, True):
                    pe.wait_ge(logit_act, 3)
                    turn_y(2, LAST, M0)
                if step == (1, 2, True):
                    pe.wait_ge(rbc_act, 2 * b)
                    logits(1, 0)
                if step == (1, 2, False):
                    pe.wait_ge(x1_dve, 2)
                    logits(1, 1)
                if step == (1, 3, True):
                    pe.wait_ge(logit_act, LC + 1)
                    logits(1, 2)
                if step == (1, 3, False):
                    pe.wait_ge(logit_act, LC + 2)
                    logits(1, 3)
                if step == (1, 4, True):
                    pe.wait_ge(logit_act, LC + 3)
                    turn_x2n(2, 2, LAST, M1)
                if step == (1, 5, True):
                    pe.wait_ge(logit_act, 2 * LC)
                    pe.wait_ge(x2nT_act, 2)
                    logits(2, 0)
                if step == (1, 5, False):
                    logits(2, 1)
                if step == (1, 6, True):
                    pe.wait_ge(logit_act, 2 * LC + 2)
                    logits(2, 2)

            def half(i, a, first=False, last=False):
                b = i * 2 + a
                ending = isinstance(i, int) and i == LAST
                for t in range(NT):
                    g = b * NT + t
                    before = not (first and t == 0)
                    u = (a + t + 1) % 2
                    if t == 0:
                        pe.wait_ge(ctxT_lo, KB * (b + 1))
                        if a == 1:
                            pe.wait_ge(qkb_lo, i + 1)
                    if a == 0:
                        pe.wait_ge(qk_lo, i * 4 + rounds_of_qk(t))
                    make_scores(g, a, t)
                    if before:
                        turn_probs(g - 1, u, 0)
                        turn_probs(g - 1, u, 1)
                    if ending:
                        early(a, t, True)
                    if first:
                        if t == 0:
                            head_products(wqT, wkT, 3, T1)
                            pe.wait_ge(wvo_in, 32)
                            turn_weight(wv_sb, 0, ACC)
                            pe.wait_ge(setup_act, 4)
                            pe.wait_ge(setup_dve, 5)
                            pe.wait_ge(qk_lo, 1)
                            make_qk(0, 2, 0)
                        if t == 1:
                            pe.wait_ge(setup_act, 5)
                            turn_weight(wv_sb, 1, ACC)
                            pe.wait_ge(qk_lo, 2)
                            make_qk(0, 3, 1)
                        if t == 2:
                            pe.wait_ge(setup_dve, 6)
                            head_products(wvT, wo_sb, 0, ACC)
                            pe.wait_ge(qk_lo, 3)
                            head_products(wvT, wo_sb, 2, M0)
                            pe.wait_ge(qk_lo, 4)
                            turn_ctx(1, 0, 1)
                        if t == 3:
                            pe.wait_ge(setup_act, 6)
                            head_products(wvT, wo_sb, 1, ACC)
                            pe.wait_ge(setup_dve, 7)
                            turn_ctx(1, 1, 0)
                            pe.wait_ge(ctxT_lo, KB + 1)
                            head_products(wvT, wo_sb, 3, M1)
                        if t == 4:
                            pe.wait_ge(setup_dve, 8)
                            turn_ctx(1, 2, 1)
                    if 1 <= t <= 3 and not first:
                        share = (b - 1, 1 - a, 1, range(4 * t - 4, 4 * t))
                    elif t >= 4 and last:
                        share = (b, a, 0, range(4 * t - 16, 4 * t - 12))
                    elif t >= 4:
                        share = (b, a, 0, range(3 * t - 12, 3 * t - 9))
                    elif t == 0 and not first:
                        share = (b - 1, 1 - a, 0, range(9, NC))
                    else:
                        share = None
                    if first and t == 4:
                        pe.wait_ge(setup_act, 7)
                    if share:
                        context_product(*share[0:3], share[3][0:-1])
                    if before:
                        turn_probs(g - 1, u, 2)
                    if share:
                        context_product(*share[0:3], share[3][-1:])
                    if a == 1 and t == 0 and not last:
                        wait(pe, y_act, i)
                        pe.wait_ge(ctxT_lo, KB * b + 2)
                        make_qk(i + 1, 0, 0)
                    if t == 1 and not first:
                        pe.wait_ge(rden_dve, b * 2)
                        pe.wait_ge(rbc_act, b * 2 - 1)
                        if ending:
                            pe.wait_ge(*((logit_act, LC) if a else (x1_dve, 1)))
                        spread_rden(1 - a, 1, a)
                    if 2 <= t <= 4 and not last and not first:
                        k = t - 2
                        if k == 2:
                            pe.wait_ge(ctxT_lo, KB * (b + 1) + 1)
                        elif k == 1:
                            wait(pe, rbc_act, b * 2)
                        elif a == 0:
                            pe.wait_ge(qk_lo, (i + 1) * 4)
                        else:
                            pe.wait_ge(qk_lo, (i + 1) * 4 + 1)
                        if ending:
                            pe.wait_ge(*((phi_cp, 2), (phi_cp, 4), (x2nT_act, 1))[k])
                        turn_ctx(b + 1, k, (1 + k + a) % 2)
                    if a == 1 and 4 <= t <= 6 and not last:
                        if t < 6:
                            pe.wait_ge(ctxT_lo, KB * (b + 1) + (t - 2))
                        else:
                            pe.wait_ge(qk_lo, (i + 1) * 4 + 2)
                        make_qk(i + 1, t - 3, (t - 3) % 2)
                    if a == 0 and t == 5 and not first:
                        pe.wait_ge(oT_dve, b * 2)
                        pe.wait_ge(ctxT_lo, KB * (b + 1) + 2)
                        if ending:
                            pe.wait_ge(logit_act, 1)
                        project(0)
                    if t == 6:
                        if a == 0 and not first:
                            project(1).then_inc(y_pe, 1)
                        pe.wait_ge(rden_dve, b * 2 + 1)
                        if a == 0:
                            pe.wait_ge(ctxT_lo, KB * (b + 1) + 3)
                            if ending:
                                pe.wait_ge(logit_act, 2)
                        elif not last:
                            pe.wait_ge(qk_lo, (i + 1) * 4 + 3)
                        else:
                            pe.wait_ge(logit_act, 2 * LC + 1)
                        spread_rden(a, 0, 1 - a)
                    if ending:
                        early(a, t, False)

            half(0, 0, first=True)
            half(0, 1)
            with pe.Fori(1, LAST) as i:
                half(i, 0)
                half(i, 1)
            half(LAST, 0)
            half(LAST, 1, last=True)

            def slots_in(q, r):
                for k in range(4 * r, 4 * r + 4):
                    last = mm(bank(SLOT_BANKS[r])[:, 128 * (k % 4):128 * (k % 4) + 128],
                              disp[q][:, 128 * k:128 * k + 128], x2n[:, q, :],
                              start=(q == 0 and k % 4 == 0), stop=(q == LAST),
                              skip_group_check=True)
                if q == LAST:
                    last.then_inc(xt_pe, 1)

            def turn_comb(q):
                pe.wait_ge(comb_pool, q + 1)
                for r in range(4):
                    if q >= 2 and r == 2:
                        pe.wait_ge(comb_dve, q - 1)
                    if q == 0:
                        pe.wait_ge(logit_act, 3 * LC + r + 1)
                    elif q == 2:
                        pe.wait_ge(xtT_act, r + 1)
                    else:
                        pe.wait_ge(combT_act, 4 * q + r - 3)
                    for c in range(4):
                        k = 4 * r + c
                        last = tr(bank(RING[r])[:, PT * c:PT * c + PT], comb[q][:, 128 * k:128 * k + 128],
                                  ident[0:PT, 0:PT])
                    last.then_inc(combT_pe, 1)

            G = B * NT
            turn_probs(G - 1, 1, 0)
            turn_probs(G - 1, 1, 1)
            pe.wait_ge(logit_act, 2 * LC + 3)
            pe.wait_ge(rden_dve, 2 * B)
            spread_rden(1, 1, 1)
            turn_probs(G - 1, 1, 2)
            context_product(B - 1, 1, 1, range(CPB), by_bank=True)
            context_product(B - 1, 1, 1, range(CPB, NC), by_bank=True)
            logits(2, 3)
            pe.wait_ge(oT_dve, 2 * B)
            project(0)
            project(1).then_inc(y_pe, 1)
            pe.wait_ge(disp_pool, 1)
            slots_in(0, 0)
            pe.wait_ge(y_act, PAIRS)
            turn_y(LAST, NQ, M0)
            slots_in(0, 1)
            pe.wait_ge(rbc_act, 2 * B)
            slots_in(0, 2)
            turn_x2n(3, LAST, NQ, M0)
            pe.wait_ge(x2nT_act, 3)
            pe.wait_ge(logit_act, 3 * LC)
            for c in range(LC):
                logits(3, c)
            slots_in(0, 3)
            pe.wait_ge(disp_pool, 2)
            for r in range(4):
                slots_in(1, r)
            pe.wait_ge(disp_pool, 3)
            for r in range(2):
                slots_in(2, r)
                pe.wait_ge(last_disp, r + 1)
                slots_in(3, r)
            turn_comb(0)
            turn_comb(1)
            slots_in(2, 2)
            slots_in(2, 3)
            pe.wait_ge(last_disp, 3)
            slots_in(3, 2)

            def turn_xt(r):
                pe.wait_ge(combT_act, 4 + r + 1)
                pe.wait_ge(tanh_act, 4 * r + 4)
                for c in range(4):
                    last = tr(bank(RING[r])[:, 128 * c:128 * c + 128], xt[:, 4 * r + c, :], ident[:, :])
                last.then_inc(xtT_pe, 1)

            def experts(r):
                pe.wait_ge(xtT_act, r + 1)
                for k in range(4 * r, 4 * r + 4):
                    for e in range(EPT):
                        p = slice(P_SLOT * e, P_SLOT * e + P_SLOT)
                        last = mm(bank(SLOT_BANKS[r])[p, 128 * (k % 4):128 * (k % 4) + 128],
                                  xtT[:, k, p], ew[:, EPT * k + e, :], start=True, stop=True)
                last.then_inc(yt_pe, 1)

            def combine(part, r):
                pe.wait_ge(yt_dve, max(r, part) + 1)
                tokens = slice(PT * PARTS[part][0], PT * PARTS[part][1])
                o = bank(SLOT_BANKS[part])[:, 0:tokens.stop - tokens.start]
                for k in range(4 * r, 4 * r + 4):
                    last = mm(o, yt[:, k, :], combT[:, k, tokens], start=(k == 0), stop=(k == NS - 1))
                if r == 3:
                    last.then_inc(y2_pe, 1)

            def turn_y2(part):
                pe.wait_ge(y2_act, part + 1)
                q0, q1 = PARTS[part]
                for q in range(q0, q1):
                    last = tr(bank(OUT_BANKS[part])[0:PT, D * (q - q0):D * (q - q0) + D],
                              y2T[:, PT * q:PT * q + PT], ident[:, :])
                last.then_inc(y2turn_pe, 1)

            pe.wait_ge(ew_in, 16)
            turn_xt(0)
            pe.wait_ge(last_disp, 4)
            slots_in(3, 3)
            experts(0)
            combine(0, 0)
            turn_xt(1)
            experts(1)
            combine(0, 1)
            turn_xt(2)
            experts(2)
            turn_xt(3)
            combine(0, 2)
            experts(3)
            turn_comb(2)
            combine(0, 3)
            turn_comb(LAST)
            for r in range(4):
                pe.wait_ge(combT_act, 8 + r + 1)
                combine(1, r)
            turn_y2(0)
            for r in range(4):
                pe.wait_ge(combT_act, 12 + r + 1)
                combine(2, r)
                if r == 1:
                    turn_y2(1)
            turn_y2(2)

        @block.scalar
        def _(act):
            act.dma_start(wq_sb[:, :], Wq).then_inc(wq_in, 16)
            act.dma_start(wk_sb[:, :], Wk).then_inc(wk_in, 16)
            act.dma_start(wv_sb[:, :], Wv).then_inc(wvo_in, 16)
            act.dma_start(wo_sb[:, :, :], Wo.rearrange("(j p) n -> p j n", p=128)).then_inc(wvo_in, 16)
            act.wait_ge(ln_var, 1)
            nc.scalar.activation(lnvar[:, :], lnvar[:, :], ACT.Sqrt).then_inc(ln_std, 1)

            def copy_out(n, dst, k, scale=None):
                act.wait_ge(setup_pe, n)
                if scale:
                    return nc.scalar.mul(dst, blocks4(bank(k)), scale).then_inc(setup_act, 1)
                return nc.scalar.copy(dst, blocks4(bank(k))).then_inc(setup_act, 1)

            def hi_ctx(b, a, k, m):
                act.wait_ge(ctxT_pe, KB * b + (k + 1))
                nc.scalar.copy(ctx_th[a][:, KW * k:KW * k + KW], misc[:, m, 0:KW]).then_inc(ctxT_hi, 1)

            def hi_qk(i, r, m):
                act.wait_ge(qk_pe, i * 4 + (r + 1))
                if r == 0:
                    wait(act, qkb_lo, i)
                both = misc[:, m, 0:4 * PT].rearrange("p (h b t) -> p b h t", h=4, b=2)
                nc.scalar.copy(qk_raw[:, 4 * r:4 * r + 4, :], both[:, 1])
                nc.scalar.copy(qk_h[0][:, 4 * r:4 * r + 4, :], both[:, 0]).then_inc(qk_hi, 1)

            def hi_probs(g, u, t, k):
                act.wait_ge(turned_pe, KB * g + (k + 1))
                nc.scalar.copy(pT_h[0:CK, t, CPB * k:CPB * k + CPB, :],
                               turned[0:CK, (KB * u + k) % 2, :].rearrange("p (c r) -> p c r", c=CPB)
                               ).then_inc(pT_hi, 1)

            def exp_tile(g, u, a, t):
                act.wait_ge(negmax_dve, g + 1)
                nc.scalar.activation(prob[u][:, :].rearrange("p (k w) -> p k w", k=KB), scores[:, :, 0:KW],
                                     ACT.Exp, bias=negmax[:, u:u + 1],
                                     accum_out=den[:, a * NT + t:a * NT + t + 1]).then_inc(exp_act, 1)

            def copy_rbc(n, grp, m):
                act.wait_ge(rbc_pe, n)
                wait(act, oT_dve, n - 1)
                w = 128 * (GROUPS[grp][1] - GROUPS[grp][0])
                nc.scalar.copy(rbc[:, 0:w], misc[:, m, 0:w]).then_inc(rbc_act, 1)

            def copy_y(i):
                act.wait_ge(y_pe, i + 1)
                nc.scalar.copy(yT[:, bass.ds(i * PT, PT)], misc[:, 0, 0:PT]).then_inc(y_act, 1)

            def copy_phi(n, k):
                act.wait_ge(phi_pe, n + 1)
                nc.scalar.copy(phiT[:, 512 * n:512 * n + 512], bank(k)).then_inc(phi_cp, 1)

            def copy_x2nT(n, q0, q1, k):
                act.wait_ge(x2nT_pe, n)
                nc.scalar.copy(x2nT[:, PT * q0:PT * q1], bank(k)[:, 0:PT * (q1 - q0)]).then_inc(x2nT_act, 1)

            def copy_logits(q, c):
                act.wait_ge(logit_pe, LC * q + c + 1)
                nc.scalar.copy(logit[q][:, 512 * c:512 * c + 512],
                               bank(LOGIT_BANKS[q][c])[0:PT, :]).then_inc(logit_act, 1)

            def copy_combT(q):
                for r in range(4):
                    act.wait_ge(combT_pe, 4 * q + r + 1)
                    nc.scalar.copy(combT[:, 4 * r:4 * r + 4, PT * q:PT * q + PT],
                                   blocks4(bank(RING[r]), PT)).then_inc(combT_act, 1)

            def dispatch_exp(q):
                act.wait_ge(dsub_pool, q + 1)
                nc.scalar.activation(disp[q][:, :], disp[q][:, :], ACT.Exp).then_inc(dexp_act, 1)

            def last_dispatch_exp(c):
                cols = slice(512 * c, 512 * c + 512)
                act.wait_ge(last_dsub, c + 1)
                nc.scalar.activation(disp[LAST][:, cols], disp[LAST][:, cols], ACT.Exp).then_inc(last_dexp, 1)

            def combine_exp(q):
                if q >= 2:
                    act.wait_ge(csub_pool, q - 1)
                else:
                    act.wait_ge(csub_dve, q + 1)
                nc.scalar.activation(comb[q][:, :], comb[q][:, :], ACT.Exp).then_inc(cexp_act, 1)

            def early(a, t, mid):
                step = (a, t, mid)
                if step == (0, 0, False):
                    copy_phi(0, M1)
                if step == (0, 1, True):
                    copy_phi(1, M1)
                if step == (0, 2, True):
                    copy_phi(2, M0)
                if step == (0, 3, True):
                    copy_phi(3, M0)
                if step == (0, 4, True):
                    copy_x2nT(1, 0, 2, M1)
                if step == (0, 5, True):
                    copy_logits(0, 0)
                if step == (0, 6, True):
                    copy_logits(0, 1)
                if step == (1, 0, True):
                    copy_logits(0, 2)
                if step == (1, 0, False):
                    copy_logits(0, 3)
                if step == (1, 2, True):
                    copy_logits(1, 0)
                if step == (1, 2, False):
                    copy_logits(1, 1)
                    dispatch_exp(0)
                if step == (1, 3, True):
                    copy_logits(1, 2)
                if step == (1, 3, False):
                    copy_logits(1, 3)
                if step == (1, 4, False):
                    combine_exp(0)
                if step == (1, 4, True):
                    copy_x2nT(2, 2, LAST, M1)
                if step == (1, 5, True):
                    copy_logits(2, 0)
                if step == (1, 5, False):
                    copy_logits(2, 1)
                if step == (1, 6, True):
                    copy_logits(2, 2)

            def half(i, a, first=False, last=False):
                b = i * 2 + a
                ending = isinstance(i, int) and i == LAST
                for t in range(NT):
                    g = b * NT + t
                    u = (a + t) % 2
                    before = not (first and t == 0)
                    if before:
                        hi_probs(g - 1, 1 - u, (t - 1) % NT, 0)
                    exp_tile(g, u, a, t)
                    if ending:
                        early(a, t, True)
                    if before:
                        hi_probs(g - 1, 1 - u, (t - 1) % NT, 1)
                        hi_probs(g - 1, 1 - u, (t - 1) % NT, 2)
                    if first:
                        if t == 0:
                            copy_out(10, wvT[:, 0:4, :], ACC)
                            hi_qk(0, 2, 0)
                        if t == 1:
                            hi_qk(0, 3, 1)
                        if t == 2:
                            copy_out(12, wvo[:, 0:8:2, :], ACC)
                            hi_ctx(1, 1, 0, 1)
                        if t == 3:
                            copy_out(14, wvo[:, 1:8:2, :], ACC)
                            hi_ctx(1, 1, 1, 0)
                        if t == 4:
                            hi_ctx(1, 1, 2, 1)
                    if a == 1 and t == 0 and not last:
                        hi_qk(i + 1, 0, 0)
                    if t == 1 and not first:
                        copy_rbc(b * 2, 1, a)
                    if 2 <= t <= 4 and not last and not first:
                        hi_ctx(b + 1, 1 - a, t - 2, (t - 1 + a) % 2)
                    if a == 1 and 4 <= t <= 6 and not last:
                        hi_qk(i + 1, t - 3, (t - 3) % 2)
                    if t == 6:
                        if a == 0 and not first:
                            copy_y(i - 1)
                        copy_rbc(b * 2 + 1, 0, 1 - a)
                    if ending:
                        early(a, t, False)

            copy_out(2, wqT[:, 4:8, :], S1)
            hi_ctx(0, 0, 0, 1)
            hi_ctx(0, 0, 1, 0)
            copy_out(5, wkT[:, 4:8, :], T0)
            hi_ctx(0, 0, 2, 1)
            copy_out(6, wqk[:, 0:8:2, :], T1, SCALE)
            hi_qk(0, 0, 0)
            hi_qk(0, 1, 1)
            copy_out(8, wqk[:, 8:16:2, :], T0, SCALE)
            half(0, 0, first=True)
            half(0, 1)
            with act.Fori(1, LAST) as i:
                half(i, 0)
                half(i, 1)
            half(LAST, 0)
            half(LAST, 1, last=True)
            G = B * NT
            hi_probs(G - 1, 1, NT - 1, 0)
            hi_probs(G - 1, 1, NT - 1, 1)
            hi_probs(G - 1, 1, NT - 1, 2)
            copy_rbc(2 * B, 1, 1)
            dispatch_exp(1)
            combine_exp(1)
            copy_logits(2, 3)
            copy_y(LAST)
            copy_x2nT(3, LAST, NQ, M0)
            dispatch_exp(2)
            copy_logits(3, 0)
            copy_logits(3, 1)
            copy_logits(3, 2)
            last_dispatch_exp(0)
            copy_logits(3, 3)
            last_dispatch_exp(1)
            last_dispatch_exp(2)
            last_dispatch_exp(3)
            copy_combT(0)
            copy_combT(1)

            def tanh_slots(r):
                act.wait_ge(nb_dve, r + 1)
                for k in range(4 * r, 4 * r + 4):
                    nc.scalar.activation(xt[:, k, :], xt[:, k, :], ACT.Tanh, bias=xt_nb[:, k:k + 1],
                                         scale=xt_rs[:, k:k + 1]).then_inc(tanh_act, 1)

            def copy_xtT(r):
                act.wait_ge(xtT_pe, r + 1)
                nc.scalar.copy(xtT[:, 4 * r:4 * r + 4, :], blocks4(bank(RING[r]))).then_inc(xtT_act, 1)

            def copy_y2(part):
                q0, q1 = PARTS[part]
                act.wait_ge(y2_pe, part + 1)
                nc.scalar.copy(y2T[:, PT * q0:PT * q1],
                               bank(SLOT_BANKS[part])[:, 0:PT * (q1 - q0)]).then_inc(y2_act, 1)

            tanh_slots(0)
            combine_exp(2)
            copy_xtT(0)
            combine_exp(LAST)
            tanh_slots(1)
            copy_xtT(1)
            tanh_slots(2)
            copy_xtT(2)
            tanh_slots(3)
            copy_xtT(3)
            copy_combT(2)
            copy_y2(0)
            copy_combT(LAST)
            copy_y2(1)
            copy_y2(2)

        @block.vector
        def _(dve):
            v = nc.vector

            def layernorm(n, src, q0, q1):
                for q in range(q0, q1):
                    s = v.bn_stats(lnbuf[:, q, :], src[:, q, :])
                s.then_inc(ln_stat, 1)
                dve.wait_ge(ln_stat, n + 1)
                for q in range(q0, q1):
                    s = v.bn_aggr(lnmv[:, q, :], lnbuf[:, q, :])
                s.then_inc(ln_mv, 1)
                dve.wait_ge(ln_mv, n + 1)
                v.tensor_scalar_add(lnvar[:, q0:q1], lnmv[:, q0:q1, 1], EPS).then_inc(ln_var, 1)
                if n == 0:
                    dve.wait_ge(ln_std, 1)
                    v.reciprocal(lnrs[:, :], lnvar[:, :]).then_inc(ln_rs, 1)

            def layernorm_apply(n, src, dst, q0, q1, done):
                dve.wait_ge(ln_rs, n + 1)
                if n == 1:
                    dve.wait_ge(qkb_lo, PAIRS)
                for q in range(q0, q1):
                    s = v.tensor_scalar(dst[:, q, :], src[:, q, :], lnmv[:, q, 0:1], lnrs[:, q:q + 1],
                                        ALU.subtract, ALU.mult)
                s.then_inc(done, 1)

            dve.wait_ge(x_in, 16)
            layernorm(0, x_sb, 0, NQ)
            layernorm_apply(0, x_sb, xn, 0, NQ, xn_ready)

            def copy_out(n, dst, k, scale=None):
                dve.wait_ge(setup_pe, n)
                if scale:
                    return v.tensor_scalar(dst, blocks4(bank(k)), scale, None, ALU.mult).then_inc(setup_dve, 1)
                return v.tensor_copy(dst, blocks4(bank(k))).then_inc(setup_dve, 1)

            def lo_ctx(b, a, k, m):
                dve.wait_ge(ctxT_hi, KB * b + (k + 1))
                cols = slice(KW * k, KW * k + KW)
                v.tensor_tensor(ctx_tl[a][:, cols], misc[:, m, 0:KW], ctx_th[a][:, cols].bitcast(F32),
                                ALU.subtract).then_inc(ctxT_lo, 1)

            def lo_qk(i, r, m):
                dve.wait_ge(qk_hi, i * 4 + (r + 1))
                both = misc[:, m, 0:4 * PT].rearrange("p (h b t) -> p b h t", h=4, b=2)
                hs = slice(4 * r, 4 * r + 4)
                v.tensor_tensor(qk_l[0][:, hs, :], both[:, 0], qk_h[0][:, hs, :].bitcast(F32),
                                ALU.subtract).then_inc(qk_lo, 1)

            def row_max(g, u):
                for k in range(KB):
                    dve.wait_ge(scores_pe, KB * g + (k + 1))
                    m = v.tensor_reduce(bankmax[:, u, k:k + 1], scores[:, k, 0:KW], AX.X, ALU.max)
                m.then_inc(bmax_dve, 1)
                dve.wait_ge(bmax_dve, g + 1)
                v.tensor_reduce(negmax[:, u:u + 1], bankmax[:, u, :], AX.X, ALU.max,
                                negate=True).then_inc(negmax_dve, 1)

            def lo_probs(g, u, t, k):
                dve.wait_ge(pT_hi, KB * g + (k + 1))
                dst = slice(CPB * k, CPB * k + CPB)
                v.tensor_tensor(pT_l[0:CK, t, dst, :],
                                turned[0:CK, (KB * u + k) % 2, :].rearrange("p (c r) -> p c r", c=CPB),
                                pT_h[0:CK, t, dst, :].bitcast(F32), ALU.subtract).then_inc(pT_lo, 1)

            def invert(g, a, grp):
                t0, t1 = GROUPS[grp]
                dve.wait_ge(exp_act, g)
                v.reciprocal(rden[:, a * NT + t0:a * NT + t1], den[:, a * NT + t0:a * NT + t1]
                             ).then_inc(rden_dve, 1)

            def normalise(n, a, grp):
                dve.wait_ge(rbc_act, n)
                dve.wait_ge(pv_pe, n)
                t0, t1 = GROUPS[grp]
                w = 128 * (t1 - t0)
                v.tensor_tensor(oT_cols[:, a, 128 * t0:128 * t1], acc[:, 0:w], rbc[:, 0:w],
                                ALU.mult).then_inc(oT_dve, 1)

            def residual(n, q0, q1, k):
                dve.wait_ge(yturn_pe, n)
                v.tensor_tensor(x_sb[:, q0:q1, :], x_sb[:, q0:q1, :],
                                bank(k)[0:PT, 0:D * (q1 - q0)].rearrange("p (q d) -> p q d", d=D),
                                ALU.add).then_inc(x1_dve, 1)
                dve.wait_ge(x1_dve, n)
                layernorm(n, x_sb, q0, q1)

            def by_expert(ap):
                return ap.rearrange("p (n s) -> p n s", s=P_SLOT)

            def by_slot(ap):
                return ap.rearrange("p (n s) -> p s n", s=P_SLOT)

            def dispatch_max(q):
                dve.wait_ge(logit_act, LC * (q + 1))
                v.tensor_reduce(dmax[q][:, :], by_expert(logit[q][:, :]), AX.X, ALU.max).then_inc(dmax_dve, 1)

            def combine_max(q):
                dve.wait_ge(logit_act, LC * (q + 1))
                v.tensor_reduce(cmax[q][:, :], by_slot(logit[q][:, :]), AX.X, ALU.max).then_inc(cmax_dve, 1)

            def combine_shift(q):
                dve.wait_ge(cmax_dve, q + 1)
                dve.wait_ge(dsub_pool, q + 1)
                v.tensor_tensor(by_expert(comb[q][:, :]), by_expert(logit[q][:, :]),
                                cmax[q][:, :].unsqueeze(1).broadcast_to([PT, N_EXP, P_SLOT]),
                                ALU.subtract).then_inc(csub_dve, 1)

            def dispatch_sum(q):
                dve.wait_ge(dexp_act, q + 1)
                v.tensor_reduce(dsum[q][:, :], by_expert(disp[q][:, :]), AX.X, ALU.add).then_inc(dsum_dve, 1)
                dve.wait_ge(dsum_dve, q + 1)
                v.reciprocal(dsum[q][:, :], dsum[q][:, :]).then_inc(drec_dve, 1)

            def combine_sum(q):
                dve.wait_ge(cexp_act, q + 1)
                v.tensor_reduce(csum[q][:, :], by_slot(comb[q][:, :]), AX.X, ALU.add).then_inc(csum_dve, 1)
                dve.wait_ge(csum_dve, q + 1)
                v.reciprocal(csum[q][:, :], csum[q][:, :]).then_inc(crec_dve, 1)

            EPB = N_EXP // LC

            def last_part(c):
                cols, experts = slice(512 * c, 512 * c + 512), slice(EPB * c, EPB * c + EPB)
                return (by_expert(logit[LAST][:, cols]), by_expert(disp[LAST][:, cols]),
                        dmax[LAST][:, experts], dsum[LAST][:, experts])

            def last_shift(c):
                lg, dp, mx, _ = last_part(c)
                dve.wait_ge(logit_act, LC * LAST + c + 1)
                v.tensor_reduce(mx, lg, AX.X, ALU.max).then_inc(last_dmax, 1)
                dve.wait_ge(last_dmax, c + 1)
                v.tensor_tensor(dp, lg, mx.unsqueeze(2).broadcast_to([PT, EPB, P_SLOT]),
                                ALU.subtract).then_inc(last_dsub, 1)

            def last_scale(c):
                _, dp, _, sm = last_part(c)
                dve.wait_ge(last_dexp, c + 1)
                v.tensor_reduce(sm, dp, AX.X, ALU.add).then_inc(last_dsum, 1)
                dve.wait_ge(last_dsum, c + 1)
                v.reciprocal(sm, sm).then_inc(last_drec, 1)
                dve.wait_ge(last_drec, c + 1)
                v.tensor_tensor(dp, dp, sm.unsqueeze(2).broadcast_to([PT, EPB, P_SLOT]),
                                ALU.mult).then_inc(last_disp, 1)

            def early(a, t):
                if (a, t) == (0, 1):
                    residual(1, 0, 2, M0)
                if (a, t) == (0, 2):
                    layernorm_apply(1, x_sb, x2n, 0, 2, x2n_dve)
                if (a, t) == (1, 1):
                    dispatch_max(0)
                if (a, t) == (1, 2):
                    residual(2, 2, LAST, M0)
                    combine_max(0)
                if (a, t) == (1, 3):
                    layernorm_apply(2, x_sb, x2n, 2, LAST, x2n_dve)
                    dispatch_sum(0)
                if (a, t) == (1, 4):
                    combine_shift(0)
                if (a, t) == (1, 5):
                    combine_sum(0)
                if (a, t) == (1, 6):
                    dispatch_max(1)

            def half(i, a, first=False, last=False):
                b = i * 2 + a
                ending = isinstance(i, int) and i == LAST
                for t in range(NT):
                    g = b * NT + t
                    u = (a + t) % 2
                    row_max(g, u)
                    if not (first and t == 0):
                        lo_probs(g - 1, 1 - u, (t - 1) % NT, 0)
                    if a == 0 and t == 0 and not first:
                        lo_qk(i, 3, 1)
                    if a == 1 and t == 1 and not last:
                        lo_qk(i + 1, 0, 0)
                    if 3 <= t <= 5 and not last and not first:
                        lo_ctx(b + 1, 1 - a, t - 3, (t - 2 + a) % 2)
                    if a == 1 and 5 <= t <= 6 and not last:
                        lo_qk(i + 1, t - 4, (t - 4) % 2)
                    if ending:
                        early(a, t)
                    if not (first and t == 0):
                        lo_probs(g - 1, 1 - u, (t - 1) % NT, 1)
                        lo_probs(g - 1, 1 - u, (t - 1) % NT, 2)
                    if first:
                        if t == 0:
                            copy_out(9, wqk[:, 9:16:2, :], T1, SCALE)
                            lo_qk(0, 2, 0)
                        if t == 1:
                            copy_out(11, wvT[:, 4:8, :], ACC)
                            lo_qk(0, 3, 1)
                        if t == 2:
                            copy_out(13, wvo[:, 8:16:2, :], M0)
                            lo_ctx(1, 1, 0, 1)
                        if t == 3:
                            lo_ctx(1, 1, 1, 0)
                            copy_out(15, wvo[:, 9:16:2, :], M1)
                        if t == 4:
                            lo_ctx(1, 1, 2, 1)
                    if t == 0 and not first:
                        normalise(b * 2 - 1, 1 - a, 0)
                        invert(b * NT, 1 - a, 1)
                    if t == 3 and not first:
                        normalise(b * 2, 1 - a, 1)
                    if t == 5:
                        invert(b * NT + 3, a, 0)

            copy_out(1, wqT[:, 0:4, :], S0)
            lo_ctx(0, 0, 0, 1)
            dve.wait_ge(setup_pe, 3)
            v.tensor_copy(xnT[:, :], bank(ACC)[:, 0:TOK]).then_inc(setup_dve, 1)
            lo_ctx(0, 0, 1, 0)
            copy_out(4, wkT[:, 0:4, :], S2)
            lo_ctx(0, 0, 2, 1)
            copy_out(7, wqk[:, 1:8:2, :], ACC, SCALE)
            lo_qk(0, 0, 0)
            lo_qk(0, 1, 1)
            half(0, 0, first=True)
            half(0, 1)
            with dve.Fori(1, LAST) as i:
                half(i, 0)
                half(i, 1)
            half(LAST, 0)
            half(LAST, 1, last=True)

            G = B * NT
            invert(G, 1, 1)
            normalise(2 * B - 1, 1, 0)
            lo_probs(G - 1, 1, NT - 1, 0)
            lo_probs(G - 1, 1, NT - 1, 1)
            lo_probs(G - 1, 1, NT - 1, 2)
            combine_max(1)
            combine_shift(1)
            dispatch_sum(1)
            normalise(2 * B, 1, 1)
            dispatch_max(2)
            combine_sum(1)
            residual(3, LAST, NQ, M0)
            layernorm_apply(3, x_sb, x2n, LAST, NQ, x2n_dve)
            combine_max(2)
            dispatch_sum(2)

            def slot_stats(r):
                ks = slice(4 * r, 4 * r + 4)
                dve.wait_ge(xt_pe, r + 1)
                v.tensor_scalar(xt[:, ks, :], blocks4(bank(SLOT_BANKS[r])), -33000.0, 65000.0,
                                ALU.max, ALU.min).then_inc(clip_dve, 1)
                dve.wait_ge(clip_dve, r + 1)
                for k in range(4 * r, 4 * r + 4):
                    s = v.bn_stats(xt_st[:, k, :], xt[:, k, :])
                s.then_inc(stat_dve, 1)
                dve.wait_ge(stat_dve, r + 1)
                for k in range(4 * r, 4 * r + 4):
                    s = v.bn_aggr(xt_mv[:, k, :], xt_st[:, k, :])
                s.then_inc(mv_dve, 1)
                dve.wait_ge(mv_dve, r + 1)
                v.tensor_scalar_add(xt_var[:, ks], xt_mv[:, ks, 1], EPS).then_inc(var_dve, 1)

            def slot_bias(r):
                ks = slice(4 * r, 4 * r + 4)
                dve.wait_ge(rs_pool, r + 1)
                v.scalar_tensor_tensor(xt_nb[:, ks], xt_mv[:, ks, 0], -1.0, xt_rs[:, ks],
                                       ALU.mult, ALU.mult).then_inc(nb_dve, 1)

            def add_expert_bias(r):
                dve.wait_ge(yt_pe, r + 1)
                v.tensor_tensor(yt[:, 4 * r:4 * r + 4, :], blocks4(bank(SLOT_BANKS[r])),
                                eb[:, 4 * r:4 * r + 4, :], ALU.add).then_inc(yt_dve, 1)

            def combine_scale_upper(q):
                dve.wait_ge(crec_dve, q + 1)
                upper = by_expert(comb[q][:, HALF:])
                v.tensor_tensor(upper, upper, csum[q][:, :].unsqueeze(1).broadcast_to([PT, N_EXP // 2, P_SLOT]),
                                ALU.mult).then_inc(comb_dve, 1)

            last_shift(0)
            last_shift(1)
            last_scale(0)
            last_shift(2)
            last_scale(1)
            last_shift(3)
            slot_stats(0)
            combine_max(LAST)
            slot_bias(0)
            last_scale(2)
            last_scale(3)
            slot_stats(1)
            dve.wait_ge(eb_in, 16 * EPT)
            add_expert_bias(0)
            slot_bias(1)
            slot_stats(2)
            slot_stats(3)
            slot_bias(2)
            add_expert_bias(1)
            slot_bias(3)
            combine_sum(2)
            combine_scale_upper(2)
            add_expert_bias(2)
            combine_sum(LAST)
            combine_scale_upper(LAST)
            add_expert_bias(3)

            for part, (q0, q1) in enumerate(PARTS):
                dve.wait_ge(y2turn_pe, part + 1)
                v.tensor_tensor(out_sb[:, q0:q1, :], x_sb[:, q0:q1, :],
                                bank(OUT_BANKS[part])[0:PT, 0:D * (q1 - q0)].rearrange("p (q d) -> p q d", d=D),
                                ALU.add).then_inc(out_dve, 1)


_INS = ['x', 'ctx_1024', 'L0_xattn_Wq', 'L0_xattn_Wk', 'L0_xattn_Wv', 'L0_xattn_Wo',
        'L0_ffn_phi_w', 'L0_ffn_phi_b', 'L0_ffn_expert_w', 'L0_ffn_expert_b']
_OUTS = [((8, 56, 128), 'float32')]


def kernel(**inputs):
    import numpy as _np
    import concourse.bacc as _bacc
    from concourse import mybir as _mybir
    from concourse.bass_utils import run_bass_kernel_spmd as _run

    nc = _bacc.Bacc("TRN2", target_bir_lowering=False, num_devices=1)
    arrays, args = {}, []
    for name in _INS:
        a = _np.ascontiguousarray(inputs[name])
        arrays[f"in_{name}_dram"] = a
        args.append(nc.dram_tensor(f"in_{name}_dram", a.shape, _mybir.dt.from_np(a.dtype), kind="ExternalInput").ap())
    for i, (shape, dtype) in enumerate(_OUTS):
        dt = _mybir.dt.from_np(_np.dtype(dtype))
        args.append(nc.dram_tensor(f"out_{i}_dram", shape, dt, kind="ExternalOutput").ap())
    xattn_softmoe_kernel(nc, *args)
    r = _run(nc, [arrays], core_ids=[0])
    got = tuple(r.results[0][f"out_{i}_dram"] for i in range(len(_OUTS)))
    return got[0]
```
